# Optimizing a Trainium2 kernel written in Bass

```python
import numpy as np
import jax
import jax.numpy as jnp

def _softmax(x, axis=-1):
    return jax.nn.softmax(x, axis=axis)

def _gelu(x):
    return jax.nn.gelu(x, approximate=True)

def _silu(x):
    return jax.nn.silu(x)

def _sigmoid(x):
    return jax.nn.sigmoid(x)

def _layernorm(x, axis=-1, eps=1e-05):
    m = jnp.mean(x, axis=axis, keepdims=True)
    v = jnp.var(x, axis=axis, keepdims=True)
    return (x - m) / jnp.sqrt(v + eps)

def _scatter_add(tgt, idx, src, axis=0):
    return tgt.at[idx].add(src)

def _segment_sum(src, seg, n):
    return jax.ops.segment_sum(src, seg, n)
kernel_name = 'mk_xattn_ffn_d2_seqx_r4_294a06'

def setup_inputs(seed: int=0):
    np.random.seed(seed)
    _w = jnp.asarray

    def _rec_inputs():
        import jax
        import jax.numpy as jnp
        _rk = jax.random.key(seed)
        x = -0.0002928 + 1 * jax.random.normal(jax.random.fold_in(_rk, 1), (1, 2048, 256), jnp.float32)
        _lenS = 2048 - jax.random.randint(jax.random.fold_in(_rk, 7), (1,), 0, max(1, 2048 // 4) + 1, jnp.int32)
        _lenS2 = 1601 - jax.random.randint(jax.random.fold_in(_rk, 8), (1,), 0, max(1, 1601 // 4) + 1, jnp.int32)
        _ctx_1024P = jax.random.normal(jax.random.fold_in(_rk, 11), (1, 16, 256), jnp.float32)
        _ctx_1024c = jax.random.dirichlet(jax.random.fold_in(_rk, 511), 0.3 * jnp.ones((16,), jnp.float32), (1, 1601))
        _ctx_1024t = jnp.einsum('bsk,bkd->bsd', _ctx_1024c, _ctx_1024P)
        _ctx_1024t = _ctx_1024t * jax.lax.rsqrt(jnp.mean(jnp.square(_ctx_1024t)) + 1e-12) * 0.953939
        ctx_1024 = -1.39393e-06 + 0.999914 * (_ctx_1024t + 0.3 * jax.random.normal(jax.random.fold_in(_rk, 611), (1, 1601, 256), jnp.float32))
        _validS = jnp.arange(2048)[None, :] < _lenS[:, None]
        _validS2 = jnp.arange(1601)[None, :] < _lenS2[:, None]
        _causal = jnp.tril(jnp.ones((2048, 2048), dtype=bool))
        mask_BxS2_bf1 = jnp.ones((1, 1601), dtype=bool)
        mask_1x1xSxS2_bk1 = jnp.broadcast_to(_validS2[0:1, None, None, :], (1, 1, 2048, 1601))
        return (x, ctx_1024, mask_BxS2_bf1, mask_1x1xSxS2_bk1)
    x, ctx_1024, mask_BxS2_bf1, mask_1x1xSxS2_bk1 = _rec_inputs()

    def _L0_xattn_setup():
        import jax, jax.numpy as jnp
        import numpy as np
        N_HEADS = 16
        D_MODEL = 256
        HEAD_DIM = D_MODEL // N_HEADS
        MASK_FILL = -100000000.0

        def _split_heads(x):
            B, S, _ = x.shape
            return x.reshape(B, S, N_HEADS, HEAD_DIM).transpose(0, 2, 1, 3)
        key = jax.random.key(seed)
        ks = jax.random.split(key, 12)
        B, L, P = (2, 512, 512)
        s = 1.0 / np.sqrt(D_MODEL).astype(np.float32)
        inp = {'q': jax.random.normal(ks[0], (B, L, D_MODEL), dtype=jnp.float32), 'k': jax.random.normal(ks[1], (B, P, D_MODEL), dtype=jnp.float32), 'v': jax.random.normal(ks[2], (B, P, D_MODEL), dtype=jnp.float32), 'attention_mask': jnp.ones((B, P), dtype=bool), 'Wq': jax.random.normal(ks[3], (D_MODEL, D_MODEL), dtype=jnp.float32) * s, 'bq': jnp.zeros((D_MODEL,), dtype=jnp.float32), 'Wk': jax.random.normal(ks[4], (D_MODEL, D_MODEL), dtype=jnp.float32) * s, 'bk': jnp.zeros((D_MODEL,), dtype=jnp.float32), 'Wv': jax.random.normal(ks[5], (D_MODEL, D_MODEL), dtype=jnp.float32) * s, 'bv': jnp.zeros((D_MODEL,), dtype=jnp.float32), 'Wo': jax.random.normal(ks[6], (D_MODEL, D_MODEL), dtype=jnp.float32) * s, 'bo': jnp.zeros((D_MODEL,), dtype=jnp.float32)}
        return inp
    _L0_xattn_all = _L0_xattn_setup()
    _L0_xattn_in = {k: v for k, v in _L0_xattn_all.items() if k in ('Wq', 'bq', 'Wk', 'bk', 'Wv', 'bv', 'Wo', 'bo')}
    del _L0_xattn_all

    def _L0_ffn_setup():
        import jax, jax.numpy as jnp
        import numpy as np
        E, G, TOPK = (32, 16, 2)
        HID, INTER, A_INTER = (256, 512, 128)
        CAP_FACTOR = 1.25
        SCALE = 0.05

        def _stats(x):
            mean = x.mean(-1, keepdims=True)
            std = jnp.std(x, axis=-1, keepdims=True, ddof=1)
            mn = x.min(-1, keepdims=True)
            mx = x.max(-1, keepdims=True)
            l2 = jnp.linalg.norm(x, axis=-1, keepdims=True)
            sp = (jnp.abs(x) < 1e-06).astype(x.dtype).mean(-1, keepdims=True)
            return jnp.concatenate([mean, std, mn, mx, l2, sp], -1)
        key = jax.random.key(seed)
        ks = jax.random.split(key, 8)
        B, N = (4, 256)
        s = lambda k, shape, sc: jax.random.normal(k, shape, jnp.float32) * sc
        return {'x': jax.random.normal(ks[0], (B, N, HID), jnp.float32), 'r1_w': s(ks[1], (HID // 2, HID + 6), 0.02), 'r1_b': jnp.zeros((HID // 2,), jnp.float32), 'r2_w': s(ks[2], (E, HID // 2), 0.02), 'w_up': s(ks[3], (E, 2 * INTER, HID), 0.02), 'w_down': s(ks[4], (E, HID, INTER), 0.02), 'a_up': s(ks[5], (G, 2 * A_INTER, HID), 0.02), 'a_down': s(ks[6], (G, HID, A_INTER), 0.02)}
    _L0_ffn_all = _L0_ffn_setup()
    _L0_ffn_in = {k: v for k, v in _L0_ffn_all.items() if k in ('r1_w', 'r1_b', 'r2_w', 'w_up', 'w_down', 'a_up', 'a_down')}
    del _L0_ffn_all

    def _L1_xattn_setup():
        import jax, jax.numpy as jnp
        import numpy as np
        D_MODEL = 256
        NUM_HEADS = 16
        D_K = D_MODEL // NUM_HEADS
        B, S = (4, 512)
        key = jax.random.key(seed)
        ks = jax.random.split(key, 12)
        sd = 1.0 / np.sqrt(D_MODEL)
        inp = {'query': jax.random.normal(ks[0], (B, S, D_MODEL), jnp.float32), 'key': jax.random.normal(ks[1], (B, S, D_MODEL), jnp.float32), 'value': jax.random.normal(ks[2], (B, S, D_MODEL), jnp.float32), 'mask': jnp.triu(jnp.ones((S, S), jnp.bool_), k=1)[None, None], 'Wq': jax.random.normal(ks[3], (D_MODEL, D_MODEL), jnp.float32) * sd, 'bq': jnp.zeros((D_MODEL,), jnp.float32), 'Wk': jax.random.normal(ks[4], (D_MODEL, D_MODEL), jnp.float32) * sd, 'bk': jnp.zeros((D_MODEL,), jnp.float32), 'Wv': jax.random.normal(ks[5], (D_MODEL, D_MODEL), jnp.float32) * sd, 'bv': jnp.zeros((D_MODEL,), jnp.float32), 'Wo': jax.random.normal(ks[6], (D_MODEL, D_MODEL), jnp.float32) * sd, 'bo': jnp.zeros((D_MODEL,), jnp.float32)}
        return inp
    _L1_xattn_all = _L1_xattn_setup()
    _L1_xattn_in = {k: v for k, v in _L1_xattn_all.items() if k in ('Wq', 'bq', 'Wk', 'bk', 'Wv', 'bv', 'Wo', 'bo')}
    del _L1_xattn_all

    def _L1_ffn_setup():
        import jax, jax.numpy as jnp
        import numpy as np
        FEATURES = 256
        D_IN = 256

        def fp8_gemm_optimized(x, input_scale, kernel, kernel_scale):
            s_in = input_scale[0]
            s_k = kernel_scale[0]
            x_q = (x.astype(jnp.float32) / s_in).astype(jnp.float8_e4m3fn)
            k_q = (kernel.astype(jnp.float32) / s_k).astype(jnp.float8_e4m3fn)
            y = jnp.dot(x_q.astype(jnp.float32), k_q.astype(jnp.float32), preferred_element_type=jnp.float32)
            return y * (s_in * s_k)
        key = jax.random.key(seed)
        kx, kk, kb = jax.random.split(key, 3)
        x = jax.random.normal(kx, (4, 2048, D_IN), dtype=jnp.float32)
        limit = np.sqrt(6.0 / (D_IN + FEATURES)).astype(np.float32)
        kernel = jax.random.uniform(kk, (D_IN, FEATURES), dtype=jnp.float32, minval=-limit, maxval=limit).astype(jnp.bfloat16)
        input_scale = jnp.ones((1,), dtype=jnp.float32)
        kernel_scale = jnp.ones((1,), dtype=jnp.float32)
        bias = jnp.zeros((FEATURES,), dtype=jnp.bfloat16)
        return {'x': x, 'kernel': kernel, 'input_scale': input_scale, 'kernel_scale': kernel_scale, 'bias': bias}
    _L1_ffn_all = _L1_ffn_setup()
    _L1_ffn_in = {k: v for k, v in _L1_ffn_all.items() if k in ('kernel', 'input_scale', 'kernel_scale', 'bias')}
    del _L1_ffn_all
    return {'x': x, 'ctx_1024': ctx_1024, 'mask_BxS2_bf1': mask_BxS2_bf1, 'mask_1x1xSxS2_bk1': mask_1x1xSxS2_bk1, 'L0_xattn_Wq': _L0_xattn_in['Wq'], 'L0_xattn_bq': _L0_xattn_in['bq'], 'L0_xattn_Wk': _L0_xattn_in['Wk'], 'L0_xattn_bk': _L0_xattn_in['bk'], 'L0_xattn_Wv': _L0_xattn_in['Wv'], 'L0_xattn_bv': _L0_xattn_in['bv'], 'L0_xattn_Wo': _L0_xattn_in['Wo'], 'L0_xattn_bo': _L0_xattn_in['bo'], 'L0_ffn_r1_w': _L0_ffn_in['r1_w'], 'L0_ffn_r1_b': _L0_ffn_in['r1_b'], 'L0_ffn_r2_w': _L0_ffn_in['r2_w'], 'L0_ffn_w_up': _L0_ffn_in['w_up'], 'L0_ffn_w_down': _L0_ffn_in['w_down'], 'L0_ffn_a_up': _L0_ffn_in['a_up'], 'L0_ffn_a_down': _L0_ffn_in['a_down'], 'L1_xattn_Wq': _L1_xattn_in['Wq'], 'L1_xattn_bq': _L1_xattn_in['bq'], 'L1_xattn_Wk': _L1_xattn_in['Wk'], 'L1_xattn_bk': _L1_xattn_in['bk'], 'L1_xattn_Wv': _L1_xattn_in['Wv'], 'L1_xattn_bv': _L1_xattn_in['bv'], 'L1_xattn_Wo': _L1_xattn_in['Wo'], 'L1_xattn_bo': _L1_xattn_in['bo'], 'L1_ffn_kernel': _L1_ffn_in['kernel'], 'L1_ffn_input_scale': _L1_ffn_in['input_scale'], 'L1_ffn_kernel_scale': _L1_ffn_in['kernel_scale'], 'L1_ffn_bias': _L1_ffn_in['bias']}

def reference(x, ctx_1024, mask_BxS2_bf1, mask_1x1xSxS2_bk1, L0_xattn_Wq, L0_xattn_bq, L0_xattn_Wk, L0_xattn_bk, L0_xattn_Wv, L0_xattn_bv, L0_xattn_Wo, L0_xattn_bo, L0_ffn_r1_w, L0_ffn_r1_b, L0_ffn_r2_w, L0_ffn_w_up, L0_ffn_w_down, L0_ffn_a_up, L0_ffn_a_down, L1_xattn_Wq, L1_xattn_bq, L1_xattn_Wk, L1_xattn_bk, L1_xattn_Wv, L1_xattn_bv, L1_xattn_Wo, L1_xattn_bo, L1_ffn_kernel, L1_ffn_input_scale, L1_ffn_kernel_scale, L1_ffn_bias):
    import jax
    import jax.numpy as jnp

    def _L0_xattn_ref(q, k, v, attention_mask, Wq, bq, Wk, bk, Wv, bv, Wo, bo):
        import jax, jax.numpy as jnp
        import numpy as np
        N_HEADS = 16
        D_MODEL = 256
        HEAD_DIM = D_MODEL // N_HEADS
        MASK_FILL = -100000000.0

        def _split_heads(x):
            B, S, _ = x.shape
            return x.reshape(B, S, N_HEADS, HEAD_DIM).transpose(0, 2, 1, 3)
        qm = _split_heads(q @ Wq.T + bq)
        km = _split_heads(k @ Wk.T + bk)
        vm = _split_heads(v @ Wv.T + bv)
        scores = jnp.einsum('bnlh,bnph->bnlp', qm, km) / np.sqrt(HEAD_DIM).astype(np.float32)
        mask = attention_mask[:, None, None, :]
        scores = jnp.where(mask, scores, MASK_FILL)
        attn = jax.nn.softmax(scores, axis=-1)
        out = jnp.einsum('bnlp,bnph->bnlh', attn, vm)
        B, _, L, _ = out.shape
        out = out.transpose(0, 2, 1, 3).reshape(B, L, D_MODEL)
        return out @ Wo.T + bo

    def _L0_ffn_ref(x, r1_w, r1_b, r2_w, w_up, w_down, a_up, a_down):
        import jax, jax.numpy as jnp
        import numpy as np
        E, G, TOPK = (32, 16, 2)
        HID, INTER, A_INTER = (256, 512, 128)
        CAP_FACTOR = 1.25
        SCALE = 0.05

        def _stats(x):
            mean = x.mean(-1, keepdims=True)
            std = jnp.std(x, axis=-1, keepdims=True, ddof=1)
            mn = x.min(-1, keepdims=True)
            mx = x.max(-1, keepdims=True)
            l2 = jnp.linalg.norm(x, axis=-1, keepdims=True)
            sp = (jnp.abs(x) < 1e-06).astype(x.dtype).mean(-1, keepdims=True)
            return jnp.concatenate([mean, std, mn, mx, l2, sp], -1)
        B, N, C = x.shape
        xf = x.reshape(-1, C)
        T = xf.shape[0]
        cap = int(CAP_FACTOR * T / E)
        ri = jnp.concatenate([xf, _stats(xf)], -1)
        h = jax.nn.gelu(ri @ r1_w.T + r1_b, approximate=False)
        probs = jax.nn.softmax(h @ r2_w.T, -1)
        topp, topi = jax.lax.top_k(probs, TOPK)
        wnorm = topp / topp.sum(-1, keepdims=True)
        eids = jnp.arange(E)
        hit = topi[..., None] == eids
        routed = hit.any(1)
        Wc = jnp.where(hit, wnorm[..., None], 0.0).sum(1)
        score = jnp.where(routed, probs, -jnp.inf)
        idx = jnp.argsort(-score, axis=0)[:cap].T
        valid = jnp.take_along_axis(routed.T, idx, 1)
        w = jnp.take_along_axis(Wc.T, idx, 1) * valid
        xe = xf[idx]
        up = jnp.einsum('eci,eji->ecj', xe, w_up)
        gate, upv = jnp.split(up, 2, axis=-1)
        hact = jax.nn.silu(gate) * upv
        ye = jnp.einsum('ecj,eoj->eco', hact, w_down)
        out = jnp.zeros((T, C), xf.dtype).at[idx.reshape(-1)].add((w[..., None] * ye).reshape(-1, C))
        Wmask = jnp.zeros((T, E), xf.dtype).at[idx, eids[:, None]].add(w)
        gw = SCALE * Wmask.reshape(T, G, E // G).sum(-1)
        aup = jnp.einsum('tc,gjc->tgj', xf, a_up)
        ag, av = jnp.split(aup, 2, axis=-1)
        ah = jax.nn.silu(ag) * av
        ay = jnp.einsum('tgj,goj->tgo', ah, a_down)
        out = out + jnp.einsum('tg,tgo->to', gw, ay)
        return out.reshape(B, N, C)

    def _L1_xattn_ref(query, key, value, mask, Wq, bq, Wk, bk, Wv, bv, Wo, bo):
        import jax, jax.numpy as jnp
        import numpy as np
        D_MODEL = 256
        NUM_HEADS = 16
        D_K = D_MODEL // NUM_HEADS
        B, S = (4, 512)
        b = query.shape[0]
        Q = query @ Wq.T + bq
        K = key @ Wk.T + bk
        V = value @ Wv.T + bv

        def split(x):
            return x.reshape(b, -1, NUM_HEADS, D_K).transpose(0, 2, 1, 3)
        Q, K, V = (split(Q), split(K), split(V))
        scores = jnp.einsum('bhqd,bhkd->bhqk', Q, K) / jnp.sqrt(jnp.float32(D_K))
        scores = jnp.where(mask, -jnp.inf, scores)
        attn_w = jax.nn.softmax(scores, axis=-1)
        attn_w = jnp.where(jnp.isnan(attn_w), 0.0, attn_w)
        out = jnp.einsum('bhqk,bhkd->bhqd', attn_w, V)
        out = out.transpose(0, 2, 1, 3).reshape(b, -1, D_MODEL)
        return out @ Wo.T + bo

    def _L1_ffn_ref(x, kernel, input_scale, kernel_scale, bias):
        import jax, jax.numpy as jnp
        import numpy as np
        FEATURES = 256
        D_IN = 256

        def fp8_gemm_optimized(x, input_scale, kernel, kernel_scale):
            s_in = input_scale[0]
            s_k = kernel_scale[0]
            x_q = (x.astype(jnp.float32) / s_in).astype(jnp.float8_e4m3fn)
            k_q = (kernel.astype(jnp.float32) / s_k).astype(jnp.float8_e4m3fn)
            y = jnp.dot(x_q.astype(jnp.float32), k_q.astype(jnp.float32), preferred_element_type=jnp.float32)
            return y * (s_in * s_k)
        dtype = jnp.bfloat16
        x = x.astype(dtype)
        orig_shape = x.shape
        x2 = x.reshape(-1, x.shape[-1])
        y = fp8_gemm_optimized(x2, input_scale, kernel, kernel_scale)
        y = y.astype(dtype) + bias
        return y.reshape(orig_shape[:-1] + (FEATURES,))
    x = x + _L0_xattn_ref(_layernorm(x, axis=-1), ctx_1024, ctx_1024, mask_BxS2_bf1, L0_xattn_Wq, L0_xattn_bq, L0_xattn_Wk, L0_xattn_bk, L0_xattn_Wv, L0_xattn_bv, L0_xattn_Wo, L0_xattn_bo)
    x = x + _L0_ffn_ref(_layernorm(x, axis=-1), L0_ffn_r1_w, L0_ffn_r1_b, L0_ffn_r2_w, L0_ffn_w_up, L0_ffn_w_down, L0_ffn_a_up, L0_ffn_a_down)
    x = x + _L1_xattn_ref(_layernorm(x, axis=-1), ctx_1024, ctx_1024, mask_1x1xSxS2_bk1, L1_xattn_Wq, L1_xattn_bq, L1_xattn_Wk, L1_xattn_bk, L1_xattn_Wv, L1_xattn_bv, L1_xattn_Wo, L1_xattn_bo)
    x = x + _L1_ffn_ref(_layernorm(x, axis=-1), L1_ffn_kernel, L1_ffn_input_scale, L1_ffn_kernel_scale, L1_ffn_bias)
    return x

_drawn_inputs = setup_inputs


def setup_inputs(seed=0):
    import zlib

    import numpy as np

    out = dict(_drawn_inputs(seed))
    spreads = {'L0_xattn_bq': (0.0, 0.391),
     'L0_xattn_bk': (0.0, 2.0),
     'L0_xattn_bv': (0.0, 0.1),
     'L0_xattn_bo': (0.0, 0.1),
     'L0_ffn_r1_b': (0.0, 0.8),
     'L1_xattn_bq': (0.0, 1.172),
     'L1_xattn_bk': (0.0, 2.0),
     'L1_xattn_bv': (0.0, 0.1),
     'L1_xattn_bo': (0.0, 0.1),
     'L1_ffn_bias': (0.0, 0.317)}
    factors = {'L0_ffn_r1_w': 5.841,
     'L0_ffn_r2_w': 5.778,
     'L0_ffn_w_up': 6.048,
     'L0_ffn_w_down': 6.05,
     'L0_ffn_a_up': 8.0,
     'L0_ffn_a_down': 8.0}
    for name, (base, spread) in spreads.items():
        noise = np.random.default_rng([zlib.crc32(name.encode()), seed]).standard_normal(out[name].shape)
        drawn = base * np.exp(spread * noise) if base else spread * noise
        out[name] = jnp.asarray(drawn.astype(out[name].dtype))
    for name, factor in factors.items():
        out[name] = (out[name] * factor).astype(out[name].dtype)
    return out
```

```python
from contextlib import ExitStack

import concourse.bass as bass
from concourse import mybir

ALU = mybir.AluOpType
ACT = mybir.ActivationFunctionType
AX = mybir.AxisListType
F32 = mybir.dt.float32
BF16 = mybir.dt.bfloat16
U8 = mybir.dt.uint8
U32 = mybir.dt.uint32
I32 = mybir.dt.int32
FP8 = mybir.dt.float8e4

P = 128
T, D = 2048, 256
NH, HD = 16, 16
S2 = 1601
TT = T // P
KT = -(-S2 // P)
KLAST = S2 - (KT - 1) * P
DH = D // P
CH = 512
QC = T // CH
HG, HPG = 4, 4
NIT = HG * QC
PASS1_ROWS = 6 * HD + 3
PASS2_ROWS = PASS1_ROWS + 3
EPS = 1e-5
Q_PART = [0, 0, 0, 1, 1, 2]
K_PART = [0, 1, 2, 0, 1, 0]
ONES_BF16_PAIR = 1.0019378662109375
MASK_FILL_PARTS = (-99614720.0, -385024.0, -256.0)
NEG_HUGE = -(2.0 ** 60)
HUGE_CUT = 2.0 ** 50
MM_LEVELS = T.bit_length() - 1

E, G, TOPK = 32, 16, 2
INTER, A_INTER = 512, 128
CAP = int(1.25 * T / E)
ROUNDS = CAP // 8
RH = D // 2
ADAPTER_SCALE = 0.05
HALL = INTER + A_INTER
TABW = D + 1
SLOTS = 4


def build(nc, a):
    scr = lambda name, shape, dt: nc.dram_tensor(name, shape, dt, kind="Internal").ap()
    dr_k = scr("dr_k", (3, D, S2), BF16)
    dr_q = scr("dr_q", (3, D, T), BF16)
    dr_m = scr("dr_m", (NIT, 3, HPG * CH), BF16)
    dr_key = scr("dr_key", (KT * P,), BF16)
    dr_tab = scr("dr_tab", (T, TABW), F32)
    dr_x = scr("dr_x", (T, D), F32)

    with ExitStack() as ctx:
        def sb(name, shape, dt):
            return ctx.enter_context(nc.sbuf_tensor(name, shape, dt))

        sems = {}

        def sem(name):
            if name not in sems:
                sems[name] = ctx.enter_context(nc.semaphore(name))
            return sems[name]

        ps = ctx.enter_context(nc.psum_tensor("ps", [P, 8, CH], F32))

        Qp = sb("Qp", [P, NH, T], BF16)
        Kp_flat = sb("Kp", [P, NH * S2], BF16)
        Kp = Kp_flat[:, :].rearrange("p (h s) -> p h s", s=S2)
        Vp = sb("Vp", [P, HG, KT * HPG, HD + 1], F32)
        R2 = sb("R2", [P, TT * D], F32)
        PB = sb("PB", [P, 4096], F32)
        OT = sb("OT", [P, NIT, CH], F32)
        wqkv = sb("wqkv", [P, 3, DH, D], F32)
        wo = sb("wo", [P, HG, D], F32)
        bvB = sb("bvB", [P, D], F32)
        boB = sb("boB", [P, D], F32)
        ident = sb("ident", [P, P], F32)
        sel = sb("sel", [P, P], F32)
        bqk = sb("bqk", [P, 2, DH], F32)
        mxs = sb("mxs", [P, 48], F32)
        negm = sb("negm", [P, 16], F32)
        mrest = sb("mrest", [16, P], F32)
        mparts = sb("mparts", [16, 3, P], BF16)
        fillc = sb("fillc", [P, 2], F32)
        expo = sb("expo", [P, 2], F32)
        neg_id = sb("neg_id", [P, P], BF16)
        mm_key = sb("mm_key", [P, KT], F32)
        mm_flag = sb("mm_flag", [P, 1, KT], BF16)
        mm_any = sb("mm_any", [P, 1], F32)
        differ = sb("differ", [P, 1], I32)

        xn = R2[:, :].rearrange("p (t d) -> p t d", d=D)
        Vg = [R2[:, b * 1664:(b + 1) * 1664].rearrange("p (u c) -> p u c", c=32) for b in range(2)]
        Pt = [PB[:, b * 1024:(b + 1) * 1024] for b in range(4)]
        OTf = OT[:, :, :].rearrange("p n c -> p (n c)")
        xnT = OTf[:, 0:DH * T].rearrange("p (k t) -> p k t", k=DH)
        ctxT = OTf[:, DH * T:DH * T + DH * S2].rearrange("p (k s) -> p k s", k=DH)
        keepB = OTf[:, DH * (T + S2):DH * (T + S2) + 802].bitcast(BF16)[:, 0:S2]
        keepU = Vp[:, :, :, :].rearrange("p a b c -> p (a b c)")[:, 1000:1402].bitcast(U8)[:, 0:S2]
        fillr = Vp[:, :, :, :].rearrange("p a b c -> p (a b c)")[:, 0:802].bitcast(BF16)[:, 0:S2]
        stg = [PB[:, s * 1792:s * 1792 + 512] for s in range(2)]
        stg_r = [PB[:, s * 1792 + 512:s * 1792 + 1024] for s in range(2)]
        stg_p = [PB[:, s * 1792 + 1024:s * 1792 + 1792].bitcast(BF16).rearrange("p (i c) -> p i c", i=3) for s in range(2)]
        lns = PB[:, 3584:4096]
        bst = lns[:, 0:96].rearrange("p (t s) -> p t s", s=6)
        lnt = [lns[:, 96 + 16 * i:112 + 16 * i] for i in range(10)]

        wq_b = wqkv[:, :, :, :].rearrange("p a b c -> p (a b c)")
        mchk = wq_b[:, 0:T // 2].bitcast(BF16)
        mtree = wq_b[:, T // 2:T // 2 + T // 4]
        mA = wq_b[:, 0:768].bitcast(BF16)
        mT = [wq_b[:, 768 + s * 256:768 + (s + 1) * 256].bitcast(BF16) for s in range(2)]
        mL = wq_b[:, 1280:1280 + 2 * KLAST].bitcast(BF16).rearrange("p (q c) -> p q c", q=4)

        QKf = Qp[:, :, :].rearrange("p h t -> p (h t)").bitcast(F32)
        x_sb = QKf[:, 0:TT * D].rearrange("p (t d) -> p t d", d=D)
        Kf = Kp_flat[:, :].bitcast(F32)
        up_w = [QKf[:, s * 3072:s * 3072 + 2048].rearrange("p (k j) -> p k j", k=2) for s in range(SLOTS)]
        dn_w = [QKf[:, s * 3072 + 2048:s * 3072 + 3072].rearrange("p (k o) -> p k o", k=4) for s in range(SLOTS)]
        aup_w = [QKf[:, 12288 + s * 768:12288 + s * 768 + 512].rearrange("p (k j) -> p k j", k=2) for s in range(2)]
        adn_w = [QKf[:, 12288 + s * 768 + 512:12288 + s * 768 + 768] for s in range(2)]
        hT = OTf[:, 4096:6144]
        xfT = OTf[:, 0:4096].rearrange("p (k t) -> p k t", k=2)
        stT = OTf[0:6, 6144:8192]
        scT = Kf[0:E, 0:2048]
        scT2 = Kf[0:E, 2048:4096]
        vals = Kf[0:E, 4096:4096 + CAP]
        idx8 = Kf[0:E, 4176:4176 + CAP].bitcast(U32)
        idxf = Kf[0:E, 4256:4256 + CAP]
        valT = Kf[0:CAP, 4336:4368]
        idxT = Kf[0:CAP, 4368:4400].bitcast(U32)
        st = Kf[:, 4400:4496].rearrange("p (t s) -> p t s", s=6)
        lg = Kf[:, 4512:5024].rearrange("p (t e) -> p t e", e=E)
        prb = Kf[:, 5024:5536].rearrange("p (t e) -> p t e", e=E)
        hit1 = Kf[:, 5536:6048].rearrange("p (t e) -> p t e", e=E)
        hit2 = Kf[:, 6048:6560].rearrange("p (t e) -> p t e", e=E)
        iot = Kf[:, 6560:7072].rearrange("p (t e) -> p t e", e=E)
        top8 = Kf[:, 7072:7200].rearrange("p (t e) -> p t e", e=8)
        topi = Kf[:, 7200:7328].bitcast(U32).rearrange("p (t e) -> p t e", e=8)
        topf = Kf[:, 7328:7360].rearrange("p (t e) -> p t e", e=2)
        den = Kf[:, 7360:7376]
        r1w = Kf[:, 7376:7376 + 256].rearrange("p (k j) -> p k j", k=2)
        r1s = Kf[0:6, 7632:7760]
        r2w = Kf[:, 7760:7792]
        r1b = Kf[:, 7792:7793]
        xe = [Kf[0:CAP, 7808 + s * TABW:7808 + (s + 1) * TABW] for s in range(4)]
        xeT = [Kf[:, 8864 + s * 160:8864 + (s + 1) * 160].rearrange("p (k c) -> p k c", k=2) for s in range(2)]
        sg = [Kf[0:CAP, 9184 + s * HALL:9184 + (s + 1) * HALL] for s in range(2)]
        hh = [PB[0:CAP, s * HALL:(s + 1) * HALL] for s in range(2)]
        hhT = [PB[:, 1280 + s * 400:1280 + (s + 1) * 400].rearrange("p (k c) -> p k c", k=5) for s in range(2)]
        ye = [PB[0:CAP, 2080 + s * D:2080 + (s + 1) * D] for s in range(2)]
        wcol = PB[0:CAP, 2592:2624]

        fk = QKf[:, 4096:4608].rearrange("p (k o) -> p k o", k=2)
        fkb = QKf[:, 4608:4864].bitcast(BF16).rearrange("p (k o) -> p k o", k=2)
        fsc = QKf[:, 4864:4868]
        fbb = QKf[:, 4868:4996].bitcast(BF16)
        fx = QKf[:, 5120:5120 + 4096]
        fa = QKf[:, 9216:9216 + 4096]
        fxb = Kf[:, 0:2048].bitcast(BF16)
        fxT = Kf[:, 2048:4096].bitcast(BF16).rearrange("p (k t) -> p k t", k=2)
        fidb = Kf[:, 4096:4160].bitcast(BF16)
        fkq = Kf[:, 4160:4416].bitcast(BF16).rearrange("p (k o) -> p k o", k=2)
        fyb = [Kf[:, 4416 + 128 * s:4544 + 128 * s].bitcast(BF16) for s in range(2)]

        def wait(eng, s, value):
            if isinstance(value, int) and value <= 0:
                return
            eng.wait_ge(s, value)

        block = ctx.enter_context(nc.Block())
        w = {n: a[n] for n in a}

        def prep_units():
            return ([("k", i) for i in range(2 * QC)] + [("v", i) for i in range(KT)]
                    + [("xt", i) for i in range(2 * QC)] + [("q", i) for i in range(2 * QC)])

        def before(pos):
            return prep_units()[pos - 8] if pos >= 8 else None

        def chunk(c):
            return c * CH, min(CH, S2 - c * CH)

        MX = []
        for i in range(HPG):
            for q in range(4):
                MX += [("A", i, q), ("B", i, q)]
            MX += [("L", i, 0)]
        NMX = len(MX)
        PER_TILE = 3
        AHEAD2 = PER_TILE * 3
        M_AT = KT - 1 - AHEAD2 // PER_TILE
        order = [(1, u) for u in range(AHEAD2, NMX)] + [(2, u) for u in range(AHEAD2)]
        MX_AT = [[] if kt == M_AT else [order.pop(0) for _ in range(PER_TILE)] for kt in range(KT)]
        NQ = HPG * 4
        PER_LAYER = {
            "ctx_in": 16, "w_in": 48, "wo_zero": 1, "wo_in": 64, "b_in": 64, "bq_set": 1,
            "var_set": 1, "rstd_set": 1, "xn_set": TT,
            "k_full": 2 * QC, "v_full": KT, "xt_full": 2 * QC, "q_full": 2 * QC,
            "k_done": 2 * QC, "v_done": KT, "xt_done": 2 * QC, "q_done": 2 * QC,
            "k_split": 2 * QC, "q_split": 2 * QC, "k_out0": 48 * QC, "k_out1": 48 * QC, "q_out0": 48 * QC, "q_out1": 48 * QC,
            "k_ones": 1, "q_ones": 1, "fill_set": 1, "fill_in": 48, "qk_in": 16 * 12, "vg_zero": 2, "vg_set": NIT,
            "mx_full": NIT * NMX, "mx_done": NIT * NMX, "negm_set": NIT, "m_full": NIT, "mc": 4 * NIT, "m_split": NIT,
            "m_out": 16 * NIT, "m_in": 16 * NIT, "sc_full": NIT * 2 * KT, "p_set": NIT * 2 * KT,
            "pv_done": NIT * KT, "ot_set": NIT, "sum_full": NIT, "inv_set": NIT, "on_set": NIT,
            "x_re": 16, "bo_add": 1, "o_full": TT, "x_add": TT}

        def moe_sync(sp):
            sp.wait_ge(sem("x_add"), TT)
            sp.dma_start(dr_x.rearrange("(t p) d -> p t d", p=P), x_sb[:, :, :]).then_inc(sem("x_saved"), 16)
            sp.dma_start(r1w, w["r1T"].rearrange("(k p) j -> p k j", p=P)).then_inc(sem("r_in"), 16)
            sp.dma_start(r1s, w["r1sT"]).then_inc(sem("r_in"), 16)
            sp.dma_start(r2w, w["r2T"]).then_inc(sem("r_in"), 16)
            sp.dma_start(r1b, w["L0_ffn_r1_b"].rearrange("(p o) -> p o", o=1)).then_inc(sem("r_in"), 16)

            def load(e, s, g, first):
                if not first:
                    sp.wait_ge(sem("dn_done"), e - SLOTS + (2 if s % 2 == 0 else 1))
                sp.dma_start(up_w[s], w["upT"][bass.ds(e, 1), :, :].rearrange("e (k p) j -> p (e k) j", p=P)).then_inc(sem(f"up_in{s}"), 16)
                sp.dma_start(dn_w[s], w["dnT"][bass.ds(e, 1), :, :].rearrange("e (k p) o -> p (e k) o", p=P)).then_inc(sem(f"dn_in{s}"), 16)
                if s % 2 == 0:
                    b = s // 2
                    sp.dma_start(aup_w[b], w["aupT"][bass.ds(g, 1), :, :].rearrange("e (k p) j -> p (e k) j", p=P)).then_inc(sem(f"a_in{b}"), 16)
                    sp.dma_start(adn_w[b], w["adnT"][bass.ds(g, 1), :, :].rearrange("e p o -> p (e o)")).then_inc(sem(f"a_in{b}"), 16)

            sp.wait_ge(sem("x_saved"), 16)
            sp.wait_ge(sem("xn_set_m"), TT)
            for s in range(SLOTS):
                load(s, s, s // 2, True)
            sp.wait_ge(sem("den_set"), 1)
            tab_v = dr_tab.rearrange("(t p) d -> p t d", p=P)
            sp.dma_start(tab_v[:, :, 0:D], xn).then_inc(sem("tab_out"), 16)
            sp.dma_start(tab_v[:, :, D:D + 1], den.rearrange("p (t o) -> p t o", o=1),
                         allow_slow_non_contiguous=True).then_inc(sem("tab_out"), 16)
            with sp.Fori(1, E // SLOTS) as r:
                for s in range(SLOTS):
                    load(r * SLOTS + s, s, r * (SLOTS // 2) + s // 2, False)
            for b in range(2):
                sp.wait_ge(sem(f"sc_done{b}"), 16 * E // 2)
            sp.dma_start(x_sb[:, :, :], dr_x.rearrange("(t p) d -> p t d", p=P)).then_inc(sem("x_back"), 16)

        def final_sync(sp):
            sp.wait_ge(sem("x_add"), 2 * TT)
            sp.dma_start(fkb, a["fk"].rearrange("(k p) o -> p k o", p=P)).then_inc(sem("f_in"), 16)
            sp.dma_start(fsc[:, 0:1], a["s_in"].partition_broadcast(P)).then_inc(sem("f_in"), 16)
            sp.dma_start(fsc[:, 1:2], a["s_k"].partition_broadcast(P)).then_inc(sem("f_in"), 16)
            sp.dma_start(fbb, a["fbias"].partition_broadcast(P)).then_inc(sem("f_in"), 16)


        @block.sync
        def _(sp):
            for L in range(2):
                pre = f"L{L}_xattn_"
                was = lambda n, L=L: L * PER_LAYER[n]
                if L == 1:
                    sp.wait_ge(sem("x_back"), 16)
                sp.dma_start(ctxT, w["ctxT"].rearrange("(k p) s -> p k s", p=P)).then_inc(sem("ctx_in"), 16)
                for i, n in enumerate(("Wk", "Wv", "Wq")):
                    sp.dma_start(wqkv[:, i, :, :], w[pre + n].rearrange("(k p) o -> p k o", p=P)).then_inc(sem("w_in"), 16)
                if L == 0:
                    x_v = w["x"].rearrange("a (t p) d -> p (a t) d", p=P)
                    for c in range(4):
                        sp.dma_start(x_sb[:, 4 * c:4 * c + 4, :], x_v[:, 4 * c:4 * c + 4, :]).then_inc(sem("x_in"), 16)
                else:
                    sp.wait_ge(sem("key_out"), 16)
                    sp.dma_start(keepB[96:P, :], dr_key[0:S2].partition_broadcast(P - 96)).then_inc(sem("left_out_in"), 16)
                sp.wait_ge(sem("wo_zero"), was("wo_zero") + 1)
                for i in range(HPG):
                    sp.dma_start(wo[32 * i:32 * i + HD, :, :],
                                 w[pre + "Wo"].rearrange("(g i d) o -> i d g o", g=HG, i=HPG)[i]).then_inc(sem("wo_in"), 16)
                for kind, dst in (("k", dr_k), ("q", dr_q)):
                    for i in range(2 * QC):
                        m, c = i // QC, i % QC
                        c0, cn = chunk(c) if kind == "k" else (c * CH, CH)
                        sp.wait_ge(sem(kind + "_split"), was(kind + "_split") + i + 1)
                        for part in range(3):
                            sp.dma_start(dst[part, m * P:(m + 1) * P, c0:c0 + cn],
                                         stg_p[i % 2][:, part, 0:cn]).then_inc(sem(f"{kind}_out{i % 2}"), 16)
                    sp.wait_ge(sem(kind + "_out0"), was(kind + "_out0") + 3 * 16 * QC)
                    sp.wait_ge(sem(kind + "_out1"), was(kind + "_out1") + 3 * 16 * QC)
                    to = Kp if kind == "k" else Qp
                    if kind == "k":
                        sp.wait_ge(sem("k_ones"), was("k_ones") + 1)
                        sp.wait_ge(sem("fill_set"), was("fill_set") + 1)
                        for part in range(3):
                            sp.dma_start(Kp[96 + part:97 + part, :, :],
                                         fillr[96 + part:97 + part, :].rearrange("p (o s) -> p o s", o=1).to_broadcast([1, NH, S2]))\
                                .then_inc(sem("fill_in"), 16)
                    else:
                        sp.wait_ge(sem("xn_set"), was("xn_set") + TT)
                    for j in range(6):
                        part = (K_PART if kind == "k" else Q_PART)[j]
                        sp.dma_start(to[HD * j:HD * (j + 1), :, :],
                                     dst[part].rearrange("(h d) t -> d h t", d=HD)).then_inc(sem("qk_in"), 16)

                with sp.Fori(0, NIT) as n:
                    sp.wait_ge(sem("m_split"), was("m_split") + n + 1)
                    sp.dma_start(dr_m[bass.ds(n, 1), :, :].rearrange("n i (u c) -> u (n i) c", c=P),
                                 mparts[:, :, :]).then_inc(sem("m_out"), 16)
                    sp.wait_ge(sem("m_out"), was("m_out") + 16 * n + 16)
                    sp.dma_start(Qp[PASS1_ROWS:PASS2_ROWS, bass.ds((n // QC) * HPG, HPG), bass.ds((n % QC) * CH, CH)],
                                 dr_m[bass.ds(n, 1), :, :].rearrange("n i (h c) -> (n i) h c", c=CH)).then_inc(sem("m_in"), 16)
                sp.wait_ge(sem("pv_done"), was("pv_done") + NIT * KT)
                sp.dma_start(x_sb, w["x"].rearrange("a (t p) d -> p (a t) d", p=P) if L == 0 else
                             dr_x.rearrange("(t p) d -> p t d", p=P)).then_inc(sem("x_re"), 16)
                if L == 0:
                    moe_sync(sp)
            final_sync(sp)
            sp.wait_ge(sem("x_out"), TT)
            sp.dma_start(a["out"].rearrange("a (t p) d -> p (a t) d", p=P), x_sb[:, :, :]).then_inc(sem("out_done"), 16)
            sp.wait_ge(sem("out_done"), 16)

        def moe_pool(pool):
            pool.wait_ge(sem("x_add"), TT)
            nc.gpsimd.iota(iot, pattern=[[0, TT], [1, E]], base=0, channel_multiplier=0,
                           allow_small_or_imprecise_dtypes=True).then_inc(sem("iota_set"), 1)
            pool.wait_ge(sem("var_set_m"), 1)
            nc.gpsimd.tensor_tensor(lnt[6], lnt[5], expo[:, 0:1].to_broadcast([P, 16]), ALU.pow).then_inc(sem("rstd_set_m"), 1)
            pool.wait_ge(sem("var2_set"), 2)
            nc.gpsimd.tensor_tensor(st[:, :, 1], lnt[7], expo[:, 1:2].to_broadcast([P, 16]), ALU.pow).then_inc(sem("root_set"), 1)
            nc.gpsimd.tensor_tensor(st[:, :, 4], lnt[8], expo[:, 1:2].to_broadcast([P, 16]), ALU.pow).then_inc(sem("root_set"), 1)
            pool.wait_ge(sem("tab_out"), 32)
            pool.wait_ge(sem("idx_set"), 2)
            pool.wait_ge(sem("x_saved"), 16)

            def gather(e):
                if e >= 4:
                    pool.wait_ge(sem("w_set"), e - 3)
                    pool.wait_ge(sem("xe_t"), e - 3)
                pool.indirect_dma_start(xe[e % 4], None, dr_tab,
                                        bass.IndirectOffsetOnAxis(ap=idxT[:, e:e + 1], axis=0)).then_inc(sem(f"xe_in{e % 4}"), 16)

            for e in range(4):
                gather(e)
            for e in range(E):
                pool.wait_ge(sem("ye_set"), e + 1)
                if e:
                    pool.wait_ge(sem(f"sc_done{(e - 1) % 2}"), 16 * ((e + 1) // 2))
                pool.indirect_dma_start(dr_x, bass.IndirectOffsetOnAxis(ap=idxT[:, e:e + 1], axis=0), ye[e % 2], None,
                                        compute_op=ALU.add).then_inc(sem(f"sc_done{e % 2}"), 16)
                if e + 4 < E:
                    gather(e + 4)

        def final_pool(pool):
            pool.wait_ge(sem("x_add"), 2 * TT)
            nc.gpsimd.tensor_copy(fidb, ident[:, :]).then_inc(sem("fidb_set"), 1)
            pool.wait_ge(sem("var_setf"), 1)
            nc.gpsimd.tensor_tensor(lnt[6], lnt[5], expo[:, 0:1].to_broadcast([P, 16]), ALU.pow).then_inc(sem("rstd_setf"), 1)

        def mask_check(pool):
            nc.gpsimd.memset(mm_key[:, :], float(T)).then_inc(sem("mm_init"), 1)
            pool.wait_ge(sem("mm_init"), 1)
            pool.wait_ge(sem("q_full"), PER_LAYER["q_full"])

            def tile(kt, kn):
                wait(pool, sem("mm_tree"), kt * MM_LEVELS)
                pool.nop(nofuse=True)
                pool.dma_start(mchk[0:kn, :], w["mask1T"][bass.ds(kt * P, kn), :]).then_inc(sem("mchk_in"), 16)
                pool.wait_ge(sem("mchk_in"), kt * 16 + 16)
                half, src = T, mchk
                for level in range(MM_LEVELS):
                    half //= 2
                    if level:
                        pool.wait_ge(sem("mm_tree"), kt * MM_LEVELS + level)
                    out = mchk[0:kn, 0:half] if level == 0 else mtree[0:kn, 0:half] if half > 1 else mm_key[0:kn, bass.ds(kt, 1)]
                    nc.gpsimd.tensor_tensor(out, src[0:kn, 0:half], src[0:kn, half:2 * half], ALU.add).then_inc(sem("mm_tree"), 1)
                    src = mchk if level == 0 else mtree

            tile(0, P)
            with pool.Fori(1, KT - 1) as kt:
                tile(kt, P)
            tile(KT - 1, KLAST)
            pool.wait_ge(sem("mm_tree"), KT * MM_LEVELS)
            nc.gpsimd.tensor_scalar(mm_flag[:, 0, :], mm_key[:, :], float(T), None, ALU.is_equal).then_inc(sem("mm_step"), 1)
            pool.wait_ge(sem("mm_step"), 1)
            nc.gpsimd.tensor_scalar(mm_key[:, :], mm_key[:, :], 0.0, None, ALU.is_equal).then_inc(sem("mm_step"), 1)
            pool.wait_ge(sem("mm_step"), 2)
            nc.gpsimd.tensor_tensor(mm_key[:, :], mm_key[:, :], mm_flag[:, 0, :], ALU.add).then_inc(sem("mm_step"), 1)
            pool.wait_ge(sem("mm_step"), 3)
            pool.dma_start(dr_key.rearrange("(t p) -> p t", p=P), mm_flag[:, 0, :],
                           allow_slow_non_contiguous=True).then_inc(sem("key_out"), 16)
            nc.gpsimd.tensor_scalar(mm_key[:, :], mm_key[:, :], -1.0, 1.0, ALU.mult, ALU.add).then_inc(sem("mm_step"), 1)
            pool.wait_ge(sem("mm_step"), 4)
            nc.gpsimd.tensor_reduce(mm_any[0:1, :], mm_key[:, :], AX.XYZWC, ALU.max).then_inc(sem("mm_step"), 1)
            pool.wait_ge(sem("mm_step"), 5)
            nc.gpsimd.tensor_copy(differ[0:1, :], mm_any[0:1, :]).then_inc(sem("differ_set"), 1)

        def mask_unit(pool, n, u):
            what, i, q = MX[u]
            rows = w["mask1"].rearrange("a b q s -> (a b q) s")
            if what == "A":
                if u:
                    last = max(v for v in range(u) if MX[v][0] == "B")
                    pool.wait_ge(sem("mx_full"), PER_LAYER["mx_full"] + n * NMX + last + 1)
                else:
                    pool.wait_ge(sem("mx_full"), PER_LAYER["mx_full"] + n * NMX)
                pool.nop(nofuse=True)
                pool.dma_start(mA, rows[bass.ds((n % QC) * CH + q * P, P), 0:3 * CH]).then_inc(sem("mA_in"), 16)
            elif what == "L" and i == 0:
                pool.wait_ge(sem("mx_full"), PER_LAYER["mx_full"] + n * NMX)
                pool.nop(nofuse=True)
                for qq in range(4):
                    pool.dma_start(mL[:, qq, :], rows[bass.ds((n % QC) * CH + qq * P, P), 3 * CH:S2]).then_inc(sem("mL_in"), 16)

        def mask_loads(pool, n, nxt, nxt2):
            for kt in range(KT):
                kn = P if kt < KT - 1 else KLAST
                pool.wait_ge(sem("sc_full"), PER_LAYER["sc_full"] + n * 2 * KT + max(0, 2 * kt - 2))
                pool.nop(nofuse=True)
                pool.dma_start(mT[kt % 2][0:kn, :], w["mask1T"][kt * P:kt * P + kn, bass.ds((n % QC) * CH, CH)])\
                    .then_inc(sem(f"mT_in{kt % 2}"), 16)
                for ahead, u in MX_AT[kt]:
                    if ahead == 1 and nxt:
                        mask_unit(pool, n + 1, u)
                    if ahead == 2 and nxt2:
                        mask_unit(pool, n + 2, u)

        @block.gpsimd
        def _(pool):
            nc.gpsimd.memset(ident[:, :], 0.0).then_inc(sem("const"), 1)
            nc.gpsimd.memset(sel[:, :], 0.0).then_inc(sem("const"), 1)
            nc.gpsimd.memset(fillc[:, :], 0.0).then_inc(sem("const"), 1)
            nc.gpsimd.memset(expo[:, 0:1], -0.5).then_inc(sem("const"), 1)
            nc.gpsimd.memset(expo[:, 1:2], 0.5).then_inc(sem("const"), 1)
            pool.wait_ge(sem("const"), 5)
            nc.gpsimd.affine_select(out=ident[:, :], in_=ident[:, :], compare_op=ALU.not_equal, fill=1.0, base=0,
                                    pattern=[[-1, P]], channel_multiplier=1).then_inc(sem("const"), 1)
            nc.gpsimd.affine_select(out=sel[:, :].rearrange("p (i c) -> p i c", c=32), in_=sel[:, :].rearrange("p (i c) -> p i c", c=32),
                                    compare_op=ALU.not_equal, fill=1.0, base=-HD,
                                    pattern=[[-32, HPG], [0, 32]], channel_multiplier=1).then_inc(sem("const"), 1)
            fills = 0
            for L, parts in enumerate((MASK_FILL_PARTS, (NEG_HUGE,))):
                for i, c in enumerate(parts):
                    nc.gpsimd.affine_select(out=fillc[:, L:L + 1], in_=fillc[:, L:L + 1], compare_op=ALU.not_equal,
                                            fill=c, base=-(96 + i), pattern=[[0, 1]], channel_multiplier=1)\
                        .then_inc(sem("fillc"), 1)
                    fills += 1
                    pool.wait_ge(sem("fillc"), fills)
            pool.wait_ge(sem("const"), 7)
            nc.gpsimd.tensor_scalar(neg_id[:, :], ident[:, :], NEG_HUGE, None, ALU.mult).then_inc(sem("neg_id_set"), 1)
            for L in range(2):
                pre = f"L{L}_xattn_"
                was = lambda n, L=L: L * PER_LAYER[n]
                if L == 1:
                    pool.wait_ge(sem("x_back"), 16)
                else:
                    pool.dma_start(keepU, w["mask0"].rearrange("b s -> (b s)").partition_broadcast(P)).then_inc(sem("keep_in"), 16)
                nc.gpsimd.memset(wo[:, :, :], 0.0).then_inc(sem("wo_zero"), 1)
                pool.dma_start(bqk[:, 0, :], w[pre + "bq"].rearrange("(m p) -> p m", p=P), allow_slow_non_contiguous=True).then_inc(sem("b_in"), 16)
                pool.dma_start(bqk[:, 1, :], w[pre + "bk"].rearrange("(m p) -> p m", p=P), allow_slow_non_contiguous=True).then_inc(sem("b_in"), 16)
                pool.dma_start(bvB[:, :], w[pre + "bv"].partition_broadcast(P)).then_inc(sem("b_in"), 16)
                pool.dma_start(boB[:, :], w[pre + "bo"].partition_broadcast(P)).then_inc(sem("b_in"), 16)
                pool.wait_ge(sem("wo_zero"), was("wo_zero") + 1)
                nc.gpsimd.memset(Kp_flat[96:P, :].bitcast(F32), ONES_BF16_PAIR).then_inc(sem("k_ones"), 1)
                pool.wait_ge(sem("k_ones"), was("k_ones") + 1)
                pool.wait_ge(sem("var_set"), was("var_set") + 1)
                nc.gpsimd.tensor_tensor(lnt[6], lnt[5], expo[:, 0:1].to_broadcast([P, TT]), ALU.pow).then_inc(sem("rstd_set"), 1)
                pool.wait_ge(sem("xn_set"), was("xn_set") + TT)
                nc.gpsimd.memset(QKf[96:P, :], ONES_BF16_PAIR).then_inc(sem("q_ones"), 1)
                pool.wait_ge(sem("q_ones"), was("q_ones") + 1)
                pool.wait_ge(sem("xt_full"), was("xt_full") + 2 * QC)
                for b in range(2):
                    nc.gpsimd.memset(Vg[b], 0.0).then_inc(sem("vg_zero"), 1)
                pool.wait_ge(sem("v_done"), was("v_done") + KT)
                pool.wait_ge(sem("vg_zero"), was("vg_zero") + 2)

                def v_copy(n, b):
                    wait(pool, sem("pv_done"), was("pv_done") + n * KT - KT)
                    nc.gpsimd.tensor_copy(Vg[b][:, :, 0:HD + 1],
                                          Vp[:, bass.ds(n // QC, 1), :, :].rearrange("p a u c -> p (a u) c")).then_inc(sem("vg_set"), 1)

                v_copy(0, 0)
                v_copy(1, 1)
                if L == 0:
                    mask_check(pool)
                    with pool.Fori(1, NIT // 2) as pair:
                        for b in range(2):
                            v_copy(2 * pair + b, b)
                else:
                    pool.wait_ge(sem("q_full"), 2 * PER_LAYER["q_full"])
                    pool.wait_ge(sem("differ_set"), 1)
                    whole = pool.value_load(differ[0:1, 0:1], min_val=0, max_val=1)
                    with pool.If(whole == 1):
                        for u in range(NMX):
                            mask_unit(pool, 0, u)
                        for u in range(AHEAD2):
                            mask_unit(pool, 1, u)
                        for n in range(2):
                            mask_loads(pool, n, True, True)
                        with pool.Fori(1, NIT // 2 - 1) as pair:
                            for b in range(2):
                                v_copy(2 * pair + b, b)
                                mask_loads(pool, 2 * pair + b, True, True)
                        v_copy(NIT - 2, 0)
                        mask_loads(pool, NIT - 2, True, False)
                        v_copy(NIT - 1, 1)
                        mask_loads(pool, NIT - 1, False, False)
                    with pool.Else():
                        with pool.Fori(1, NIT // 2) as pair:
                            for b in range(2):
                                v_copy(2 * pair + b, b)
                if L == 0:
                    moe_pool(pool)
            final_pool(pool)

        def moe_pe(pe):
            pe.wait_ge(sem("x_add"), TT)
            for i in range(2 * QC):
                h, c = i % DH, i // DH
                pe.wait_ge(sem("xn_set_m"), 4 * c + 4)
                for j in range(4):
                    mm = nc.tensor.transpose(ps[:, i, j * P:(j + 1) * P], xn[:, 4 * c + j, h * P:(h + 1) * P], ident[:, :])
                mm.then_inc(sem("xt_full_m"), 1)
            pe.wait_ge(sem("xt_done_m"), 2 * QC)
            pe.wait_ge(sem("st_set"), 3)
            pe.wait_ge(sem("root_set"), 2)
            for c in range(QC):
                for j in range(4):
                    mm = nc.tensor.transpose(ps[0:6, c, j * P:(j + 1) * P], st[:, 4 * c + j, :], ident[:, :])
                mm.then_inc(sem("stt_full"), 1)
            pe.wait_ge(sem("r_in"), 64)
            for c in range(QC):
                pe.wait_ge(sem("stt_done"), c + 1)
                for k in range(DH):
                    nc.tensor.matmul(ps[:, 4 + c, :], r1w[:, k, :], xfT[:, k, c * CH:(c + 1) * CH], start=(k == 0), stop=False)
                nc.tensor.matmul(ps[:, 4 + c, :], r1s, stT[:, c * CH:(c + 1) * CH], start=False, stop=True).then_inc(sem("rh_full"), 1)
            for t in range(TT):
                pe.wait_ge(sem("rh_set"), t // 4 + 1)
                mm = nc.tensor.matmul(ps[:, 0, t * E:(t + 1) * E], hT[:, t * P:(t + 1) * P], r2w, start=True, stop=True)
            mm.then_inc(sem("lg_full"), 1)
            pe.wait_ge(sem("score_set"), 1)
            for t in range(TT):
                mm = nc.tensor.transpose(ps[0:E, 1 + t // 4, (t % 4) * P:(t % 4 + 1) * P], prb[:, t, :], ident[:, :])
            mm.then_inc(sem("sct_full"), 1)
            pe.wait_ge(sem("top_set"), 1)
            nc.tensor.transpose(ps[0:CAP, 5, 0:E], vals, ident[0:E, 0:E])
            nc.tensor.transpose(ps[0:CAP, 5, E:2 * E], idxf, ident[0:E, 0:E]).then_inc(sem("topT_full"), 1)

            def up(r, s):
                b = s % 2
                e = r * SLOTS + s
                pe.wait_ge(sem(f"xe_in{s}"), 16 * r + 16)
                wait(pe, sem("xeT_set"), e)
                for k in range(DH):
                    mm = nc.tensor.transpose(ps[:, 5, k * CAP:(k + 1) * CAP], xe[s][:, k * P:(k + 1) * P], ident[0:CAP, 0:CAP])
                mm.then_inc(sem("xe_t"), 1)
                pe.wait_ge(sem("xeT_set"), e + 1)
                pe.wait_ge(sem(f"up_in{s}"), 16 * r + 16)
                pe.wait_ge(sem(f"a_in{s // 2}"), 32 * r + 32)
                wait(pe, sem(f"hh_set{b}"), r * 2 + s // 2)
                for j, bank in ((0, b), (1, 2 + b)):
                    for k in range(DH):
                        nc.tensor.matmul(ps[0:CAP, bank, :], xeT[b][:, k, :], up_w[s][:, k, j * CH:(j + 1) * CH],
                                         start=(k == 0), stop=(k == DH - 1))
                wait(pe, sem(f"hh_set{1 - b}"), r * 2 + (s + 1) // 2)
                for k in range(DH):
                    mm = nc.tensor.matmul(ps[0:CAP, 4, 0:2 * A_INTER], xeT[b][:, k, :], aup_w[s // 2][:, k, :],
                                          start=(k == 0), stop=(k == DH - 1))
                mm.then_inc(sem("up_full"), 1)

            def down(r, s):
                b = s % 2
                e = r * SLOTS + s
                pe.wait_ge(sem(f"hh_set{b}"), r * 2 + s // 2 + 1)
                wait(pe, sem("hhT_set"), e)
                for k in range(5):
                    mm = nc.tensor.transpose(ps[:, 6, k * CAP:(k + 1) * CAP], hh[b][:, k * P:(k + 1) * P], ident[0:CAP, 0:CAP])
                mm.then_inc(sem("hhT_full"), 1)
                pe.wait_ge(sem("hhT_set"), e + 1)
                pe.wait_ge(sem(f"dn_in{s}"), 16 * r + 16)
                wait(pe, sem("ye_set"), e)
                for k in range(5):
                    mm = nc.tensor.matmul(ps[0:CAP, 7, 0:D], hhT[b][:, k, :], dn_w[s][:, k, :] if k < 4 else adn_w[s // 2],
                                          start=(k == 0), stop=(k == 4))
                mm.then_inc(sem("dn_done"), 1)

            def round_(r, last):
                for s in range(SLOTS):
                    if s < SLOTS - 1:
                        up(r, s + 1)
                    elif not last:
                        up(r + 1, 0)
                    down(r, s)

            pe.wait_ge(sem("idx_set"), 2)
            up(0, 0)
            round_(0, False)
            with pe.Fori(1, E // SLOTS - 1) as r:
                round_(r, False)
            round_(E // SLOTS - 1, True)

        def final_pe(pe):
            pe.wait_ge(sem("fidb_set"), 1)
            pe.wait_ge(sem("x_add"), 2 * TT)
            for c in range(QC):
                pe.wait_ge(sem("fx_set"), c + 1)
                bank = ps[:, c, :].bitcast(BF16)
                for k in range(DH):
                    for j in range(4):
                        mm = nc.tensor.transpose(bank[:, k * CH + j * P:k * CH + (j + 1) * P],
                                                 fxb[:, (4 * c + j) * D + k * P:(4 * c + j) * D + (k + 1) * P], fidb)
                mm.then_inc(sem("fxT_full"), 1)
            pe.wait_ge(sem("fk_set"), 1)
            for t in range(TT):
                pe.wait_ge(sem("fxT_set"), t // 4 + 1)
                if t >= 4:
                    pe.wait_ge(sem("x_out"), t - 3)
                for k in range(DH):
                    mm = nc.tensor.matmul(ps[:, 4 + t % 4, 0:D], fxT[:, k, t * P:(t + 1) * P], fkq[:, k, :],
                                          start=(k == 0), stop=(k == DH - 1))
                mm.then_inc(sem("y_full"), 1)

        @block.tensor
        def _(pe):
            pe.wait_ge(sem("const"), 7)
            for L in range(2):
                was = lambda n, L=L: L * PER_LAYER[n]
                pe.wait_ge(sem("ctx_in"), was("ctx_in") + 16)
                pe.wait_ge(sem("w_in"), was("w_in") + 48)
                for pos, (kind, i) in enumerate(prep_units()):
                    bank = pos % 8
                    if before(pos):
                        k2, i2 = before(pos)
                        pe.wait_ge(sem(k2 + "_done"), was(k2 + "_done") + i2 + 1)
                    if kind == "k":
                        m, c = i // QC, i % QC
                        c0, cn = chunk(c)
                        for k in range(DH):
                            mm = nc.tensor.matmul(ps[:, bank, 0:cn], wqkv[:, 0, k, m * P:(m + 1) * P],
                                                  ctxT[:, k, c0:c0 + cn], start=(k == 0), stop=(k == DH - 1))
                    elif kind == "v":
                        kn = P if i < KT - 1 else KLAST
                        for k in range(DH):
                            mm = nc.tensor.matmul(ps[0:kn, bank, 0:D], ctxT[:, k, i * P:i * P + kn],
                                                  wqkv[:, 1, k, :], start=(k == 0), stop=(k == DH - 1))
                    elif kind == "xt":
                        h, c = i % DH, i // DH
                        pe.wait_ge(sem("xn_set"), was("xn_set") + 4 * c + 4)
                        for j in range(4):
                            mm = nc.tensor.transpose(ps[:, bank, j * P:(j + 1) * P], xn[:, 4 * c + j, h * P:(h + 1) * P], ident[:, :])
                    else:
                        m, c = i // QC, i % QC
                        pe.wait_ge(sem("xt_done"), was("xt_done") + (DH * (c + 1) if m == 0 else DH * QC))
                        for k in range(DH):
                            mm = nc.tensor.matmul(ps[:, bank, :], wqkv[:, 2, k, m * P:(m + 1) * P],
                                                  xnT[:, k, c * CH:(c + 1) * CH], start=(k == 0), stop=(k == DH - 1))
                    mm.then_inc(sem(kind + "_full"), 1)
                pe.wait_ge(sem("q_done"), was("q_done") + 2 * QC)
                pe.wait_ge(sem("v_done"), was("v_done") + KT)
                pe.wait_ge(sem("fill_in"), was("fill_in") + 48)
                pe.wait_ge(sem("qk_in"), was("qk_in") + 16 * 12)
                pe.wait_ge(sem("q_ones"), was("q_ones") + 1)

                def scores(out, lhsT, rhs, mask, kn, masked):
                    mm = nc.tensor.matmul(out, lhsT, rhs, start=True, stop=not masked)
                    if masked:
                        mm = nc.tensor.matmul(out, neg_id[0:kn, 0:kn], mask, start=False, stop=True)
                    return mm

                def mx_unit(n, u, masked):
                    what, i, q = MX[u]
                    g, qc = n // QC, n % QC
                    h = g * HPG + i
                    prev = [v for v in range(u) if (MX[v][0] == "A") == (what == "A")]
                    if prev:
                        pe.wait_ge(sem("mx_done"), was("mx_done") + n * NMX + prev[-1] + 1)
                    else:
                        wait(pe, sem("mx_done"), was("mx_done") + n * NMX)
                        if what == "B" and not (isinstance(n, int) and n == 0):
                            pe.wait_ge(sem("mc"), was("mc") + n * 4 - 3)
                    Kh = lambda c0, cn: Kp[0:PASS1_ROWS, bass.ds(h, 1), c0:c0 + cn].rearrange("p a b -> p (a b)")
                    Qh = lambda qq: Qp[0:PASS1_ROWS, bass.ds(h, 1), bass.ds(qc * CH + qq * P, P)].rearrange("p a b -> p (a b)")
                    if what == "A":
                        if masked:
                            pe.wait_ge(sem("mA_in"), 16 * (n * NQ + i * 4 + q + 1))
                        for j in range(2):
                            mm = scores(ps[:, 4 + j, :], Qh(q), Kh(j * CH, CH), mA[:, j * CH:(j + 1) * CH], P, masked)
                    elif what == "B":
                        mm = scores(ps[:, 6, :], Qh(q), Kh(2 * CH, CH), mA[:, 2 * CH:3 * CH], P, masked)
                    else:
                        if masked:
                            pe.wait_ge(sem("mL_in"), 64 * (n + 1))
                        for qq in range(4):
                            mm = scores(ps[:, 6, qq * KLAST:(qq + 1) * KLAST], Qh(qq), Kh(3 * CH, KLAST), mL[:, qq, :], P, masked)
                    mm.then_inc(sem("mx_full"), 1)

                def m_transpose(n):
                    pe.wait_ge(sem("negm_set"), was("negm_set") + n + 1)
                    nc.tensor.transpose(ps[0:16, 6, 0:P], negm[:, :], ident[:, :]).then_inc(sem("m_full"), 1)

                def pv(n, b, kt):
                    kn = P if kt < KT - 1 else KLAST
                    pe.wait_ge(sem("p_set"), was("p_set") + n * 2 * KT + 2 * kt + 2)
                    if kt == 0:
                        pe.wait_ge(sem("vg_set"), was("vg_set") + n + 1)
                        wait(pe, sem("ot_set"), was("ot_set") + n)
                    for i in range(HPG):
                        mm = nc.tensor.matmul(ps[32 * i:32 * i + 32, 7, :], Vg[b][0:kn, kt * HPG + i, :],
                                              Pt[(2 * (KT * b + kt) + i // 2) % 4][0:kn, (i % 2) * CH:(i % 2 + 1) * CH],
                                              start=(kt == 0), stop=(kt == KT - 1))
                    mm.then_inc(sem("pv_done"), 1)

                def iteration(n, b, nxt, nxt2, masked):
                    g, qc = n // QC, n % QC
                    pe.wait_ge(sem("m_in"), was("m_in") + 16 * n + 16)
                    for kt in range(KT):
                        kn = P if kt < KT - 1 else KLAST
                        if masked:
                            pe.wait_ge(sem(f"mT_in{kt % 2}"), 16 * (n * ((KT + 1 - kt % 2) // 2) + kt // 2 + 1))
                        for half in range(2):
                            v = 2 * kt + half
                            wait(pe, sem("p_set"), was("p_set") + n * 2 * KT + v - 1)
                            for i in (2 * half, 2 * half + 1):
                                h = g * HPG + i
                                mm = scores(ps[0:kn, 2 * (v % 2) + i % 2, :],
                                            Kp[0:PASS2_ROWS, bass.ds(h, 1), kt * P:kt * P + kn].rearrange("p a b -> p (a b)"),
                                            Qp[0:PASS2_ROWS, bass.ds(h, 1), bass.ds(qc * CH, CH)].rearrange("p a b -> p (a b)"),
                                            mT[kt % 2][0:kn, :], kn, masked)
                            mm.then_inc(sem("sc_full"), 1)
                        for ahead, u in MX_AT[kt]:
                            if ahead == 1 and nxt:
                                mx_unit(n + 1, u, masked)
                            if ahead == 2 and nxt2:
                                mx_unit(n + 2, u, masked)
                        if kt == M_AT and nxt:
                            m_transpose(n + 1)
                        if kt:
                            pv(n, b, kt - 1)
                    pv(n, b, KT - 1)

                def iterations(masked):
                    for u in range(NMX):
                        mx_unit(0, u, masked)
                    m_transpose(0)
                    for u in range(AHEAD2):
                        mx_unit(1, u, masked)
                    iteration(0, 0, True, True, masked)
                    iteration(1, 1, True, True, masked)
                    with pe.Fori(1, NIT // 2 - 1) as pair:
                        for b in range(2):
                            iteration(2 * pair + b, b, True, True, masked)
                    iteration(NIT - 2, 0, True, False, masked)
                    iteration(NIT - 1, 1, False, False, masked)

                if L == 0:
                    iterations(False)
                else:
                    pe.wait_ge(sem("neg_id_set"), 1)
                    pe.wait_ge(sem("differ_set"), 1)
                    whole = pe.value_load(differ[0:1, 0:1], min_val=0, max_val=1)
                    with pe.If(whole == 1):
                        iterations(True)
                    with pe.Else():
                        iterations(False)

                for n in range(NIT):
                    bank = n % 4
                    pe.wait_ge(sem("ot_set"), was("ot_set") + n + 1)
                    if n >= 4:
                        pe.wait_ge(sem("inv_set"), was("inv_set") + n - 3)
                    else:
                        pe.wait_ge(sem("p_set"), was("p_set") + NIT * 2 * KT)
                    nc.tensor.matmul(ps[:, bank, :], sel[:, :], OT[:, n, :], start=True, stop=True).then_inc(sem("sum_full"), 1)
                pe.wait_ge(sem("wo_in"), was("wo_in") + 64)
                pe.wait_ge(sem("on_set"), was("on_set") + NIT)
                pe.wait_ge(sem("mx_done"), was("mx_done") + NIT * NMX)
                for t in range(TT):
                    bank = 4 + t % 4
                    wait(pe, sem("x_add"), was("x_add") + t - 3)
                    for g in range(HG):
                        mm = nc.tensor.matmul(ps[:, bank, 0:D], OT[:, g * QC + t // 4, (t % 4) * P:(t % 4 + 1) * P],
                                              wo[:, g, :], start=(g == 0), stop=(g == HG - 1))
                    mm.then_inc(sem("o_full"), 1)
                if L == 0:
                    moe_pe(pe)
            final_pe(pe)

        def moe_act(act):
            for i in range(2 * QC):
                h, c = i % DH, i // DH
                act.wait_ge(sem("xt_full_m"), i + 1)
                nc.scalar.activation(xfT[:, h, c * CH:(c + 1) * CH], ps[:, i, :], ACT.Copy).then_inc(sem("xt_done_m"), 1)
            act.wait_ge(sem("r_in"), 64)
            for c in range(QC):
                act.wait_ge(sem("rh_full"), c + 1)
                nc.scalar.activation(hT[:, c * CH:(c + 1) * CH], ps[:, 4 + c, :], ACT.Gelu, bias=r1b).then_inc(sem("rh_set"), 1)
            act.wait_ge(sem("lg_sub"), 1)
            nc.scalar.activation(lg.rearrange("p t e -> p (t e)"), lg.rearrange("p t e -> p (t e)"), ACT.Exp).then_inc(sem("lg_exp"), 1)

            def silu(r, s):
                b = s % 2
                e = r * SLOTS + s
                act.wait_ge(sem("up_full"), e + 1)
                wait(act, sem(f"hh_set{b}"), r * 2 + s // 2)
                nc.scalar.activation(sg[b][:, 0:INTER], ps[0:CAP, b, :], ACT.Silu)
                nc.scalar.activation(sg[b][:, INTER:HALL], ps[0:CAP, 4, 0:A_INTER], ACT.Silu).then_inc(sem("silu_set"), 1)

            for s in range(SLOTS):
                silu(0, s)
            with act.Fori(1, E // SLOTS) as r:
                for s in range(SLOTS):
                    silu(r, s)

        def final_act(act):
            for c in range(QC):
                act.wait_ge(sem("fxT_full"), c + 1)
                nc.scalar.activation(fxT[:, :, c * CH:(c + 1) * CH],
                                     ps[:, c, :].bitcast(BF16).rearrange("p (k t) -> p k t", k=2), ACT.Copy).then_inc(sem("fxT_set"), 1)

        @block.scalar
        def _(act):
            for L in range(2):
                was = lambda n, L=L: L * PER_LAYER[n]
                act.wait_ge(sem("b_in"), was("b_in") + 64)
                nc.scalar.mul(bqk[:, 0, :], bqk[:, 0, :], HD ** -0.5).then_inc(sem("bq_set"), 1)
                act.wait_ge(sem("bq_set"), was("bq_set") + 1)
                for pos, (kind, i) in enumerate(prep_units()):
                    bank = pos % 8
                    if kind == "v":
                        continue
                    act.wait_ge(sem(kind + "_full"), was(kind + "_full") + i + 1)
                    if kind == "xt":
                        h, c = i % DH, i // DH
                        nc.scalar.activation(xnT[:, h, c * CH:(c + 1) * CH], ps[:, bank, :], ACT.Copy).then_inc(sem("xt_done"), 1)
                        continue
                    m, c = i // QC, i % QC
                    cn = chunk(c)[1] if kind == "k" else CH
                    if i >= 2:
                        act.wait_ge(sem(kind + "_split"), was(kind + "_split") + i - 1)
                    elif kind == "q":
                        act.wait_ge(sem("k_split"), was("k_split") + 2 * QC)
                    nc.scalar.activation(stg[i % 2][:, 0:cn], ps[:, bank, 0:cn], ACT.Identity,
                                         bias=bqk[:, 1 if kind == "k" else 0, m:m + 1],
                                         scale=1.0 if kind == "k" else HD ** -0.5).then_inc(sem(kind + "_done"), 1)
                act.wait_ge(sem("q_split"), was("q_split") + 2 * QC)
                act.wait_ge(sem("q_out0"), was("q_out0") + 3 * 16 * QC)
                act.wait_ge(sem("q_out1"), was("q_out1") + 3 * 16 * QC)

                def exps(n, b):
                    for kt in range(KT):
                        kn = P if kt < KT - 1 else KLAST
                        for half in range(2):
                            v = 2 * kt + half
                            buf = (2 * KT * b + v) % 4
                            act.wait_ge(sem("sc_full"), was("sc_full") + n * 2 * KT + v + 1)
                            wait(act, sem("pv_done"), was("pv_done") + n * KT + kt - 1)
                            nc.scalar.activation(Pt[buf][0:kn, :], ps[0:kn, 2 * (v % 2):2 * (v % 2) + 2, :].rearrange("p b c -> p (b c)"),
                                                 ACT.Exp).then_inc(sem("p_set"), 1)

                exps(0, 0)
                exps(1, 1)
                with act.Fori(1, NIT // 2) as pair:
                    for b in range(2):
                        exps(2 * pair + b, b)
                if L == 0:
                    moe_act(act)
            final_act(act)

        def ln_stats(dve, link, src, var_sem, rstd_sem, out_sem, rstd_count=1):
            for t in range(TT):
                ins = nc.vector.bn_stats(bst[:, t, :], src[:, t, :])
            link(ins)
            link(nc.vector.tensor_tensor(lnt[0], bst[:, :, 1], bst[:, :, 4], ALU.add))
            nc.vector.tensor_tensor(lnt[2], bst[:, :, 1], bst[:, :, 4], ALU.subtract)
            link(nc.vector.tensor_tensor(lnt[3], bst[:, :, 2], bst[:, :, 5], ALU.add))
            link(nc.vector.tensor_tensor(lnt[4], lnt[2], lnt[2], ALU.mult))
            link(nc.vector.scalar_tensor_tensor(lnt[4], lnt[4], 64.0, lnt[3], ALU.mult, ALU.add))
            nc.vector.tensor_scalar(lnt[1], lnt[0], 0.5, None, ALU.mult)
            nc.vector.tensor_scalar(lnt[5], lnt[4], 1.0 / D, EPS, ALU.mult, ALU.add).then_inc(var_sem, 1)
            dve.wait_ge(rstd_sem, rstd_count)
            for t in range(TT):
                nc.vector.tensor_scalar(xn[:, t, :], src[:, t, :], lnt[1][:, t:t + 1], lnt[6][:, t:t + 1],
                                        ALU.subtract, ALU.mult).then_inc(out_sem, 1)

        def split(dve, link, was, kind, i, L):
            s = i % 2
            m, c = i // QC, i % QC
            cn = chunk(c)[1] if kind == "k" else CH
            dve.wait_ge(sem(kind + "_done"), was(kind + "_done") + i + 1)
            if kind == "k" and L == 0:
                link(nc.vector.tensor_tensor(stg[s][:, 0:cn], stg[s][:, 0:cn], keepB[:, chunk(c)[0]:chunk(c)[0] + cn], ALU.mult))
            if i >= 2:
                dve.wait_ge(sem(f"{kind}_out{s}"), was(f"{kind}_out{s}") + 48 * (i // 2))
            elif kind == "q":
                dve.wait_ge(sem(f"k_out{s}"), was(f"k_out{s}") + 48 * QC)
            link(nc.vector.tensor_copy(stg_p[s][:, 0, 0:cn], stg[s][:, 0:cn]))
            link(nc.vector.tensor_tensor(stg_r[s][:, 0:cn], stg[s][:, 0:cn], stg_p[s][:, 0, 0:cn], ALU.subtract))
            link(nc.vector.tensor_copy(stg_p[s][:, 1, 0:cn], stg_r[s][:, 0:cn]))
            nc.vector.tensor_tensor(stg_p[s][:, 2, 0:cn], stg_r[s][:, 0:cn], stg_p[s][:, 1, 0:cn], ALU.subtract)\
                .then_inc(sem(kind + "_split"), 1)

        def moe_dve(dve, link):
            dve.wait_ge(sem("x_add"), TT)
            ln_stats(dve, link, x_sb, sem("var_set_m"), sem("rstd_set_m"), sem("xn_set_m"))
            dve.wait_ge(sem("xn_set_m"), TT)
            for t in range(TT):
                ins = nc.vector.bn_stats(bst[:, t, :], xn[:, t, :])
            link(ins)
            nc.vector.tensor_tensor(lnt[2], bst[:, :, 1], bst[:, :, 4], ALU.subtract)
            nc.vector.tensor_tensor(lnt[3], bst[:, :, 2], bst[:, :, 5], ALU.add)
            link(nc.vector.tensor_tensor(lnt[0], bst[:, :, 1], bst[:, :, 4], ALU.add))
            link(nc.vector.tensor_tensor(lnt[4], lnt[2], lnt[2], ALU.mult))
            link(nc.vector.scalar_tensor_tensor(lnt[4], lnt[4], 64.0, lnt[3], ALU.mult, ALU.add))
            link(nc.vector.tensor_scalar(st[:, :, 0], lnt[0], 0.5, None, ALU.mult))
            link(nc.vector.tensor_tensor(lnt[9], st[:, :, 0], st[:, :, 0], ALU.mult))
            nc.vector.scalar_tensor_tensor(lnt[8], lnt[9], float(D), lnt[4], ALU.mult, ALU.add).then_inc(sem("var2_set"), 1)
            nc.vector.tensor_scalar(lnt[7], lnt[4], 1.0 / (D - 1), None, ALU.mult).then_inc(sem("var2_set"), 1)
            nc.vector.tensor_reduce(st[:, :, 2], xn, AX.X, ALU.min).then_inc(sem("st_set"), 1)
            nc.vector.tensor_reduce(st[:, :, 3], xn, AX.X, ALU.max).then_inc(sem("st_set"), 1)
            for t0, t1 in ((0, 14), (14, TT)):
                near = PB[:, 0:(t1 - t0) * D]
                link(nc.vector.tensor_scalar(near, R2[:, t0 * D:t1 * D], -1e-6, None, ALU.is_gt))
                link(nc.vector.scalar_tensor_tensor(near, R2[:, t0 * D:t1 * D], 1e-6, near, ALU.is_lt, ALU.mult))
                link(nc.vector.tensor_reduce(lnt[9][:, t0:t1], near.rearrange("p (t d) -> p t d", d=D), AX.X, ALU.add))
            nc.vector.tensor_scalar(st[:, :, 5], lnt[9], 1.0 / D, None, ALU.mult).then_inc(sem("st_set"), 1)
            for c in range(QC):
                dve.wait_ge(sem("stt_full"), c + 1)
                nc.vector.tensor_copy(stT[:, c * CH:(c + 1) * CH], ps[0:6, c, :]).then_inc(sem("stt_done"), 1)
            dve.wait_ge(sem("lg_full"), 1)
            lgp = ps[:, 0, :].rearrange("p (t e) -> p t e", e=E)
            bc = lambda v: v.rearrange("p (t o) -> p t o", o=1).to_broadcast([P, TT, E])
            link(nc.vector.tensor_reduce(lnt[0], lgp, AX.X, ALU.max))
            nc.vector.tensor_tensor(lg, lgp, bc(lnt[0]), ALU.subtract).then_inc(sem("lg_sub"), 1)
            dve.wait_ge(sem("lg_exp"), 1)
            link(nc.vector.tensor_reduce(lnt[1], lg, AX.X, ALU.add))
            link(nc.vector.reciprocal(lnt[2], lnt[1]))
            link(nc.vector.tensor_tensor(prb, lg, bc(lnt[2]), ALU.mult))
            for t in range(TT):
                ins = nc.vector.max(top8[:, t, :], prb[:, t, :])
            link(ins)
            for t in range(TT):
                ins = nc.vector.max_index(topi[:, t, :], top8[:, t, :], prb[:, t, :])
            link(ins)
            link(nc.vector.tensor_tensor(den, top8[:, :, 0], top8[:, :, 1], ALU.add))
            nc.vector.reciprocal(den, den).then_inc(sem("den_set"), 1)
            link(nc.vector.tensor_copy(topf, topi[:, :, 0:2]))
            dve.wait_ge(sem("iota_set"), 1)
            nc.vector.tensor_tensor(hit1, iot, topf[:, :, 0:1].to_broadcast([P, TT, E]), ALU.is_equal)
            link(nc.vector.tensor_tensor(hit2, iot, topf[:, :, 1:2].to_broadcast([P, TT, E]), ALU.is_equal))
            link(nc.vector.tensor_tensor(hit1, hit1, hit2, ALU.add))
            link(nc.vector.tensor_tensor(prb, prb, hit1, ALU.mult))
            nc.vector.scalar_tensor_tensor(prb, hit1, -1.0, prb, ALU.add, ALU.add).then_inc(sem("score_set"), 1)
            dve.wait_ge(sem("sct_full"), 1)
            link(nc.vector.tensor_copy(scT, ps[0:E, 1:5, :].rearrange("p b c -> p (b c)")))
            src, dst = scT, scT2
            for r in range(ROUNDS):
                link(nc.vector.max(vals[:, 8 * r:8 * r + 8], src))
                ins = nc.vector.max_index(idx8[:, 8 * r:8 * r + 8], vals[:, 8 * r:8 * r + 8], src)
                if r < ROUNDS - 1:
                    ins = nc.vector.match_replace(dst, vals[:, 8 * r:8 * r + 8], src, -2.0)
                link(ins)
                src, dst = dst, src
            nc.vector.tensor_copy(idxf, idx8).then_inc(sem("top_set"), 1)
            dve.wait_ge(sem("topT_full"), 1)
            nc.vector.tensor_scalar(valT, ps[0:CAP, 5, 0:E], 0.0, None, ALU.max).then_inc(sem("idx_set"), 1)
            nc.vector.tensor_copy(idxT, ps[0:CAP, 5, E:2 * E]).then_inc(sem("idx_set"), 1)
            dve.wait_ge(sem("idx_set"), 2)

            def rows(r, s):
                e = r * SLOTS + s
                dve.wait_ge(sem(f"xe_in{s}"), 16 * r + 16)
                nc.vector.tensor_tensor(wcol[:, s:s + 1], valT[:, bass.ds(e, 1)], xe[s][:, D:D + 1], ALU.mult).then_inc(sem("w_set"), 1)
                dve.wait_ge(sem("xe_t"), e + 1)
                nc.vector.tensor_copy(xeT[s % 2], ps[:, 5, 0:2 * CAP].rearrange("p (k c) -> p k c", k=2)).then_inc(sem("xeT_set"), 1)

            def hidden(r, s):
                b = s % 2
                e = r * SLOTS + s
                dve.wait_ge(sem("silu_set"), e + 1)
                nc.vector.tensor_tensor(hh[b][:, 0:INTER], sg[b][:, 0:INTER], ps[0:CAP, 2 + b, :], ALU.mult)
                nc.vector.scalar_tensor_tensor(hh[b][:, INTER:HALL], ps[0:CAP, 4, A_INTER:2 * A_INTER], ADAPTER_SCALE,
                                               sg[b][:, INTER:HALL], ALU.mult, ALU.mult).then_inc(sem(f"hh_set{b}"), 1)
                dve.wait_ge(sem("hhT_full"), e + 1)
                nc.vector.tensor_copy(hhT[b], ps[:, 6, 0:5 * CAP].rearrange("p (k c) -> p k c", k=5)).then_inc(sem("hhT_set"), 1)
                dve.wait_ge(sem("dn_done"), e + 1)
                dve.wait_ge(sem("w_set"), e + 1)
                wait(dve, sem(f"sc_done{b}"), 16 * (r * 2 + s // 2))
                nc.vector.tensor_scalar(ye[b], ps[0:CAP, 7, 0:D], wcol[:, s:s + 1], None, ALU.mult).then_inc(sem("ye_set"), 1)

            def round_(r, last):
                for s in range(SLOTS):
                    if s < SLOTS - 1:
                        rows(r, s + 1)
                    elif not last:
                        rows(r + 1, 0)
                    hidden(r, s)

            rows(0, 0)
            round_(0, False)
            with dve.Fori(1, E // SLOTS - 1) as r:
                round_(r, False)
            round_(E // SLOTS - 1, True)

        def final_dve(dve, link):
            def round_fp8(v, t1, out):
                link(nc.vector.tensor_scalar(t1.bitcast(I32), v.bitcast(I32), 0x7F800000, None, ALU.bitwise_and))
                link(nc.vector.tensor_scalar(t1, t1, 2.0 ** -6, 1.5 * 2.0 ** 20, ALU.max, ALU.mult))
                link(nc.vector.tensor_tensor(v, v, t1, ALU.add))
                link(nc.vector.tensor_tensor(v, v, t1, ALU.subtract))
                link(nc.vector.tensor_scalar(t1.bitcast(I32), v.bitcast(I32), 0x7FFFFFFF, None, ALU.bitwise_and))
                link(nc.vector.tensor_scalar(t1, t1, 2.0 ** 119, 0.2 * 2.0 ** 127, ALU.mult, ALU.add))
                return nc.vector.scalar_tensor_tensor(out, t1, 0.0, v, ALU.mult, ALU.add)

            dve.wait_ge(sem("x_add"), 2 * TT)
            ln_stats(dve, link, x_sb, sem("var_setf"), sem("rstd_setf"), sem("xn_setf"))
            dve.wait_ge(sem("f_in"), 16 * 4)
            link(nc.vector.tensor_tensor(fsc[:, 2:3], fsc[:, 0:1], fsc[:, 1:2], ALU.mult))
            link(nc.vector.reciprocal(fsc[:, 0:2], fsc[:, 0:2]))
            link(nc.vector.tensor_tensor(fk.rearrange("p k o -> p (k o)"), fkb.rearrange("p k o -> p (k o)"), fsc[:, 1:2].to_broadcast([P, 2 * D]), ALU.mult))
            round_fp8(fk.rearrange("p k o -> p (k o)"), fa[:, 0:512], fkq.rearrange("p k o -> p (k o)")).then_inc(sem("fk_set"), 1)
            dve.wait_ge(sem("fk_set"), 1)
            dve.wait_ge(sem("xn_setf"), TT)
            NPC = 4
            w4 = TT * D // NPC
            for c in range(NPC):
                part = slice(c * w4, (c + 1) * w4)
                link(nc.vector.tensor_copy(fxb[:, part], R2[:, part]))
                link(nc.vector.tensor_tensor(fx[:, part], fxb[:, part], fsc[:, 0:1].to_broadcast([P, w4]), ALU.mult))
                round_fp8(fx[:, part], fa[:, part], fxb[:, part]).then_inc(sem("fx_set"), 1)
            for t in range(TT):
                yb = fyb[t % 2]
                dve.wait_ge(sem("y_full"), t + 1)
                link(nc.vector.tensor_scalar(yb, ps[:, 4 + t % 4, 0:D], fsc[:, 2:3], None, ALU.mult))
                link(nc.vector.tensor_tensor(yb, yb, fbb, ALU.add))
                nc.vector.tensor_tensor(x_sb[:, t, :], x_sb[:, t, :], yb, ALU.add).then_inc(sem("x_out"), 1)

        @block.vector
        def _(dve):
            cnt = [0]

            def link(ins):
                cnt[0] += 1
                ins.then_inc(sem("dve_chain"), 1)
                dve.wait_ge(sem("dve_chain"), cnt[0])

            for L in range(2):
                was = lambda n, L=L: L * PER_LAYER[n]
                if L == 0:
                    dve.wait_ge(sem("keep_in"), 16)
                    dve.wait_ge(sem("fillc"), 4)
                    link(nc.vector.tensor_copy(keepB, keepU))
                    link(nc.vector.tensor_scalar(fillr[96:P, :], keepB[96:P, :], -1.0, 1.0, ALU.mult, ALU.add))
                    nc.vector.tensor_scalar(fillr[96:P, :], fillr[96:P, :], fillc[96:P, L:L + 1], None, ALU.mult).then_inc(sem("fill_set"), 1)
                    dve.wait_ge(sem("x_in"), 64)
                else:
                    dve.wait_ge(sem("left_out_in"), 16)
                    nc.vector.tensor_scalar(fillr[96:P, :], keepB[96:P, :], fillc[96:P, L:L + 1], None, ALU.mult).then_inc(sem("fill_set"), 1)
                    dve.wait_ge(sem("x_back"), 16)
                ln_stats(dve, link, x_sb, sem("var_set"), sem("rstd_set"), sem("xn_set"), L + 1)
                for i in range(2 * QC):
                    split(dve, link, was, "k", i, L)
                dve.wait_ge(sem("b_in"), was("b_in") + 64)
                dve.wait_ge(sem("fill_in"), was("fill_in") + 48)
                link(nc.vector.memset(Vp[:, :, :, :], 1.0))
                for i in range(KT):
                    kn = P if i < KT - 1 else KLAST
                    pos = prep_units().index(("v", i))
                    dve.wait_ge(sem("v_full"), was("v_full") + i + 1)
                    for g in range(HG):
                        ins = nc.vector.tensor_tensor(
                            Vp[0:kn, g, i * HPG:(i + 1) * HPG, 0:HD],
                            ps[0:kn, pos % 8, g * 64:(g + 1) * 64].rearrange("p (u c) -> p u c", c=HD),
                            bvB[0:kn, g * 64:(g + 1) * 64].rearrange("p (u c) -> p u c", c=HD), ALU.add)
                    ins.then_inc(sem("v_done"), 1)
                for i in range(2 * QC):
                    split(dve, link, was, "q", i, L)

                def mx_red(n, u):
                    what, i, q = MX[u]
                    dve.wait_ge(sem("mx_full"), was("mx_full") + n * NMX + u + 1)
                    if what == "A":
                        ins = nc.vector.tensor_reduce(mxs[:, i * 4 + q:i * 4 + q + 1], ps[:, 4:6, :].rearrange("p b c -> p (b c)"), AX.X, ALU.max)
                    elif what == "B":
                        ins = nc.vector.tensor_reduce(mxs[:, 16 + i * 4 + q:16 + i * 4 + q + 1], ps[:, 6, :], AX.X, ALU.max)
                    else:
                        ins = nc.vector.tensor_reduce(mxs[:, 32 + i * 4:32 + i * 4 + 4],
                                                      ps[:, 6, 0:4 * KLAST].rearrange("p (q c) -> p q c", c=KLAST), AX.X, ALU.max)
                    ins.then_inc(sem("mx_done"), 1)

                def m_split(n):
                    dve.wait_ge(sem("mx_done"), was("mx_done") + n * NMX + NMX)
                    nc.vector.tensor_reduce(negm[:, :], mxs[:, :].rearrange("p (w u) -> p u w", w=3), AX.X, ALU.max,
                                            negate=True).then_inc(sem("negm_set"), 1)
                    dve.wait_ge(sem("m_full"), was("m_full") + n + 1)
                    wait(dve, sem("m_out"), was("m_out") + 16 * n)
                    c4 = n * 4
                    nc.vector.tensor_scalar(mrest[:, :], ps[0:16, 6, 0:P], HUGE_CUT, None, ALU.min).then_inc(sem("mc"), 1)
                    dve.wait_ge(sem("mc"), was("mc") + c4 + 1)
                    nc.vector.tensor_copy(mparts[:, 0, :], mrest[:, :]).then_inc(sem("mc"), 1)
                    dve.wait_ge(sem("mc"), was("mc") + c4 + 2)
                    nc.vector.tensor_tensor(mrest[:, :], mrest[:, :], mparts[:, 0, :], ALU.subtract).then_inc(sem("mc"), 1)
                    dve.wait_ge(sem("mc"), was("mc") + c4 + 3)
                    nc.vector.tensor_copy(mparts[:, 1, :], mrest[:, :]).then_inc(sem("mc"), 1)
                    dve.wait_ge(sem("mc"), was("mc") + c4 + 4)
                    nc.vector.tensor_tensor(mparts[:, 2, :], mrest[:, :], mparts[:, 1, :], ALU.subtract).then_inc(sem("m_split"), 1)

                def evac(n):
                    dve.wait_ge(sem("pv_done"), was("pv_done") + n * KT + KT)
                    nc.vector.tensor_copy(OT[:, bass.ds(n, 1), :].rearrange("p a c -> p (a c)"), ps[:, 7, :]).then_inc(sem("ot_set"), 1)

                for u in range(NMX):
                    mx_red(0, u)
                m_split(0)
                for u in range(AHEAD2):
                    mx_red(1, u)

                def iteration(n, nxt, nxt2):
                    if nxt:
                        for u in range(AHEAD2, NMX):
                            mx_red(n + 1, u)
                        m_split(n + 1)
                    if nxt2:
                        for u in range(AHEAD2):
                            mx_red(n + 2, u)
                    evac(n)

                with dve.Fori(0, NIT - 2) as n:
                    iteration(n, True, True)
                iteration(NIT - 2, True, False)
                iteration(NIT - 1, False, False)
                for n in range(NIT):
                    dve.wait_ge(sem("sum_full"), was("sum_full") + n + 1)
                    rc = PB[:, (n % 2) * CH:(n % 2 + 1) * CH]
                    link(nc.vector.tensor_scalar(rc, ps[:, n % 4, :], 1e-30, None, ALU.max))
                    rr = PB[:, (2 + n % 2) * CH:(3 + n % 2) * CH]
                    nc.vector.reciprocal(rr, rc).then_inc(sem("inv_set"), 1)
                    dve.wait_ge(sem("inv_set"), was("inv_set") + n + 1)
                    nc.vector.tensor_tensor(OT[:, n, :], OT[:, n, :], rr, ALU.mult).then_inc(sem("on_set"), 1)
                dve.wait_ge(sem("x_re"), was("x_re") + 16)
                nc.vector.tensor_tensor(x_sb, x_sb, boB[:, :].rearrange("p (o d) -> p o d", o=1).to_broadcast([P, TT, D]), ALU.add)\
                    .then_inc(sem("bo_add"), 1)
                dve.wait_ge(sem("bo_add"), was("bo_add") + 1)
                for t in range(TT):
                    dve.wait_ge(sem("o_full"), was("o_full") + t + 1)
                    nc.vector.tensor_tensor(x_sb[:, t, :], x_sb[:, t, :], ps[:, 4 + t % 4, 0:D], ALU.add).then_inc(sem("x_add"), 1)
                if L == 0:
                    moe_dve(dve, link)
            final_dve(dve, link)

_T = {"L0_ffn_w_up": "upT", "L0_ffn_w_down": "dnT", "L0_ffn_a_up": "aupT", "L0_ffn_a_down": "adnT"}


def laid_out(inputs):
    import numpy as np
    got = {"x": inputs["x"], "ctxT": inputs["ctx_1024"][0].T, "mask0": inputs["mask_BxS2_bf1"],
           "mask1": inputs["mask_1x1xSxS2_bk1"], "mask1T": inputs["mask_1x1xSxS2_bk1"][0, 0].T}
    for L in range(2):
        for n in "qkvo":
            got[f"L{L}_xattn_W{n}"] = inputs[f"L{L}_xattn_W{n}"].T
            got[f"L{L}_xattn_b{n}"] = inputs[f"L{L}_xattn_b{n}"]
    got["r1T"] = inputs["L0_ffn_r1_w"][:, :D].T
    got["r1sT"] = inputs["L0_ffn_r1_w"][:, D:].T
    got["r2T"] = inputs["L0_ffn_r2_w"].T
    got["L0_ffn_r1_b"] = inputs["L0_ffn_r1_b"]
    for n, t in _T.items():
        got[t] = inputs[n].transpose(0, 2, 1)
    got["fk"] = inputs["L1_ffn_kernel"]
    got["s_in"] = inputs["L1_ffn_input_scale"]
    got["s_k"] = inputs["L1_ffn_kernel_scale"]
    got["fbias"] = inputs["L1_ffn_bias"]
    return {n: np.ascontiguousarray(v) for n, v in got.items()}


def kernel(**inputs):
    import concourse.bacc as _bacc
    from concourse import mybir as _mybir
    from concourse.bass_utils import run_bass_kernel_spmd as _run

    nc = _bacc.Bacc("TRN2", target_bir_lowering=False, num_devices=1)
    arrays, args = {}, {}
    for name, v in laid_out(inputs).items():
        arrays[f"in_{name}_dram"] = v
        args[name] = nc.dram_tensor(f"in_{name}_dram", v.shape, _mybir.dt.from_np(v.dtype), kind="ExternalInput").ap()
    args["out"] = nc.dram_tensor("out_0_dram", (1, T, D), F32, kind="ExternalOutput").ap()
    build(nc, args)
    r = _run(nc, [arrays], core_ids=[0])
    return r.results[0]["out_0_dram"]
```

```python
from contextlib import ExitStack

import concourse.bass as bass
from concourse import mybir

ALU = mybir.AluOpType
ACT = mybir.ActivationFunctionType
AX = mybir.AxisListType
F32 = mybir.dt.float32
BF16 = mybir.dt.bfloat16
U8 = mybir.dt.uint8
U32 = mybir.dt.uint32
I32 = mybir.dt.int32
FP8 = mybir.dt.float8e4

P = 128
T, D = 2048, 256
NH, HD = 16, 16
S2 = 1601
TT = T // P
KT = -(-S2 // P)
KLAST = S2 - (KT - 1) * P
DH = D // P
CH = 512
QC = T // CH
HG, HPG = 4, 4
NIT = HG * QC
PASS1_ROWS = 6 * HD + 3
PASS2_ROWS = PASS1_ROWS + 3
EPS = 1e-5
Q_PART = [0, 0, 0, 1, 1, 2]
K_PART = [0, 1, 2, 0, 1, 0]
ONES_BF16_PAIR = 1.0019378662109375
MASK_FILL_PARTS = (-99614720.0, -385024.0, -256.0)
NEG_HUGE = -(2.0 ** 60)
HUGE_CUT = 2.0 ** 50
MM_LEVELS = T.bit_length() - 1

E, G, TOPK = 32, 16, 2
INTER, A_INTER = 512, 128
CAP = int(1.25 * T / E)
ROUNDS = CAP // 8
RH = D // 2
ADAPTER_SCALE = 0.05
HALL = INTER + A_INTER
TABW = D + 1
SLOTS = 4


def build(nc, a):
    scr = lambda name, shape, dt: nc.dram_tensor(name, shape, dt, kind="Internal").ap()
    dr_k = scr("dr_k", (3, D, S2), BF16)
    dr_q = scr("dr_q", (3, D, T), BF16)
    dr_m = scr("dr_m", (NIT, 3, HPG * CH), BF16)
    dr_key = scr("dr_key", (KT * P,), BF16)
    dr_tab = scr("dr_tab", (T, TABW), F32)
    dr_x = scr("dr_x", (T, D), F32)

    with ExitStack() as ctx:
        def sb(name, shape, dt):
            return ctx.enter_context(nc.sbuf_tensor(name, shape, dt))

        sems = {}

        def sem(name):
            if name not in sems:
                sems[name] = ctx.enter_context(nc.semaphore(name))
            return sems[name]

        ps = ctx.enter_context(nc.psum_tensor("ps", [P, 8, CH], F32))

        Qp = sb("Qp", [P, NH, T], BF16)
        Kp_flat = sb("Kp", [P, NH * S2], BF16)
        Kp = Kp_flat[:, :].rearrange("p (h s) -> p h s", s=S2)
        Vp = sb("Vp", [P, HG, KT * HPG, HD + 1], F32)
        R2 = sb("R2", [P, TT * D], F32)
        PB = sb("PB", [P, 4096], F32)
        OT = sb("OT", [P, NIT, CH], F32)
        wqkv = sb("wqkv", [P, 3, DH, D], F32)
        wo = sb("wo", [P, HG, D], F32)
        bvB = sb("bvB", [P, D], F32)
        boB = sb("boB", [P, D], F32)
        ident = sb("ident", [P, P], F32)
        sel = sb("sel", [P, P], F32)
        bqk = sb("bqk", [P, 2, DH], F32)
        mxs = sb("mxs", [P, 48], F32)
        negm = sb("negm", [P, 16], F32)
        mrest = sb("mrest", [16, P], F32)
        mparts = sb("mparts", [16, 3, P], BF16)
        fillc = sb("fillc", [P, 2], F32)
        tiny = sb("tiny", [P, 1], F32)
        expo = sb("expo", [P, 2], F32)
        neg_id = sb("neg_id", [P, P], BF16)
        mm_key = sb("mm_key", [P, KT], F32)
        mm_flag = sb("mm_flag", [P, 1, KT], BF16)
        mm_any = sb("mm_any", [P, 1], F32)
        differ = sb("differ", [P, 1], I32)

        xn = R2[:, :].rearrange("p (t d) -> p t d", d=D)
        Vg = [R2[:, b * 1664:(b + 1) * 1664].rearrange("p (u c) -> p u c", c=32) for b in range(2)]
        rsum = R2[:, 3328:3328 + CH]
        Pt = [PB[:, b * 1024:(b + 1) * 1024] for b in range(4)]
        OTf = OT[:, :, :].rearrange("p n c -> p (n c)")
        xnT = OTf[:, 0:DH * T].rearrange("p (k t) -> p k t", k=DH)
        ctxT = OTf[:, DH * T:DH * T + DH * S2].rearrange("p (k s) -> p k s", k=DH)
        keepB = OTf[:, DH * (T + S2):DH * (T + S2) + 802].bitcast(BF16)[:, 0:S2]
        keepU = Vp[:, :, :, :].rearrange("p a b c -> p (a b c)")[:, 1000:1402].bitcast(U8)[:, 0:S2]
        fillr = Vp[:, :, :, :].rearrange("p a b c -> p (a b c)")[:, 0:802].bitcast(BF16)[:, 0:S2]
        stg = [PB[:, s * 1792:s * 1792 + 512] for s in range(2)]
        stg_r = [PB[:, s * 1792 + 512:s * 1792 + 1024] for s in range(2)]
        stg_p = [PB[:, s * 1792 + 1024:s * 1792 + 1792].bitcast(BF16).rearrange("p (i c) -> p i c", i=3) for s in range(2)]
        lns = PB[:, 3584:4096]
        bst = lns[:, 0:96].rearrange("p (t s) -> p t s", s=6)
        lnt = [lns[:, 96 + 16 * i:112 + 16 * i] for i in range(10)]

        wq_b = wqkv[:, :, :, :].rearrange("p a b c -> p (a b c)")
        mchk = wq_b[:, 0:T // 2].bitcast(BF16)
        mtree = wq_b[:, T // 2:T // 2 + T // 4]
        mA = wq_b[:, 0:768].bitcast(BF16)
        mT = [wq_b[:, 768 + s * 256:768 + (s + 1) * 256].bitcast(BF16) for s in range(2)]
        mL = wq_b[:, 1280:1280 + 2 * KLAST].bitcast(BF16).rearrange("p (q c) -> p q c", q=4)

        QKf = Qp[:, :, :].rearrange("p h t -> p (h t)").bitcast(F32)
        x_sb = QKf[:, 0:TT * D].rearrange("p (t d) -> p t d", d=D)
        Kf = Kp_flat[:, :].bitcast(F32)
        up_w = [QKf[:, s * 3072:s * 3072 + 2048].rearrange("p (k j) -> p k j", k=2) for s in range(SLOTS)]
        dn_w = [QKf[:, s * 3072 + 2048:s * 3072 + 3072].rearrange("p (k o) -> p k o", k=4) for s in range(SLOTS)]
        aup_w = [QKf[:, 12288 + s * 768:12288 + s * 768 + 512].rearrange("p (k j) -> p k j", k=2) for s in range(2)]
        adn_w = [QKf[:, 12288 + s * 768 + 512:12288 + s * 768 + 768] for s in range(2)]
        hT = OTf[:, 4096:6144]
        xfT = OTf[:, 0:4096].rearrange("p (k t) -> p k t", k=2)
        stT = OTf[0:6, 6144:8192]
        scT = Kf[0:E, 0:2048]
        scT2 = Kf[0:E, 2048:4096]
        vals = Kf[0:E, 4096:4096 + CAP]
        idx8 = Kf[0:E, 4176:4176 + CAP].bitcast(U32)
        idxf = Kf[0:E, 4256:4256 + CAP]
        valT = Kf[0:CAP, 4336:4368]
        idxT = Kf[0:CAP, 4368:4400].bitcast(U32)
        st = Kf[:, 4400:4496].rearrange("p (t s) -> p t s", s=6)
        lg = Kf[:, 4512:5024].rearrange("p (t e) -> p t e", e=E)
        prb = Kf[:, 5024:5536].rearrange("p (t e) -> p t e", e=E)
        hit1 = Kf[:, 5536:6048].rearrange("p (t e) -> p t e", e=E)
        hit2 = Kf[:, 6048:6560].rearrange("p (t e) -> p t e", e=E)
        iot = Kf[:, 6560:7072].rearrange("p (t e) -> p t e", e=E)
        top8 = Kf[:, 7072:7200].rearrange("p (t e) -> p t e", e=8)
        topi = Kf[:, 7200:7328].bitcast(U32).rearrange("p (t e) -> p t e", e=8)
        topf = Kf[:, 7328:7360].rearrange("p (t e) -> p t e", e=2)
        den = Kf[:, 7360:7376]
        r1w = Kf[:, 7376:7376 + 256].rearrange("p (k j) -> p k j", k=2)
        r1s = Kf[0:6, 7632:7760]
        r2w = Kf[:, 7760:7792]
        r1b = Kf[:, 7792:7793]
        xe = [Kf[0:CAP, 7808 + s * TABW:7808 + (s + 1) * TABW] for s in range(4)]
        xeT = [Kf[:, 8864 + s * 160:8864 + (s + 1) * 160].rearrange("p (k c) -> p k c", k=2) for s in range(2)]
        sg = [Kf[0:CAP, 9184 + s * HALL:9184 + (s + 1) * HALL] for s in range(2)]
        hh = [PB[0:CAP, s * HALL:(s + 1) * HALL] for s in range(2)]
        hhT = [PB[:, 1280 + s * 400:1280 + (s + 1) * 400].rearrange("p (k c) -> p k c", k=5) for s in range(2)]
        ye = [PB[0:CAP, 2080 + s * D:2080 + (s + 1) * D] for s in range(2)]
        wcol = PB[0:CAP, 2592:2624]

        fk = QKf[:, 4096:4608].rearrange("p (k o) -> p k o", k=2)
        fkb = QKf[:, 4608:4864].bitcast(BF16).rearrange("p (k o) -> p k o", k=2)
        fsc = QKf[:, 4864:4868]
        fbb = QKf[:, 4868:4996].bitcast(BF16)
        fx = QKf[:, 5120:5120 + 4096]
        fa = QKf[:, 9216:9216 + 4096]
        fxb = Kf[:, 0:2048].bitcast(BF16)
        fxT = Kf[:, 2048:4096].bitcast(BF16).rearrange("p (k t) -> p k t", k=2)
        fidb = Kf[:, 4096:4160].bitcast(BF16)
        fkq = Kf[:, 4160:4416].bitcast(BF16).rearrange("p (k o) -> p k o", k=2)
        fyb = [Kf[:, 4416 + 128 * s:4544 + 128 * s].bitcast(BF16) for s in range(2)]

        def wait(eng, s, value):
            if isinstance(value, int) and value <= 0:
                return
            eng.wait_ge(s, value)

        block = ctx.enter_context(nc.Block())
        w = {n: a[n] for n in a}

        def prep_units():
            return ([("k", i) for i in range(2 * QC)] + [("xt", i) for i in range(2 * QC)]
                    + [("q", i) for i in range(2 * QC)] + [("v", i) for i in range(KT)])

        def before(pos):
            return prep_units()[pos - 8] if pos >= 8 else None

        def chunk(c):
            return c * CH, min(CH, S2 - c * CH)

        MX = []
        for i in range(HPG):
            for q in range(4):
                MX += [("A", i, q), ("B", i, q)]
            MX += [("L", i, 0)]
        NMX = len(MX)
        PER_TILE = 3
        AHEAD2 = PER_TILE * 2
        M_AT = KT - 1 - AHEAD2 // PER_TILE
        order = [(1, u) for u in range(AHEAD2, NMX)] + [(2, u) for u in range(AHEAD2)]
        MX_AT = [[] if kt == M_AT else [order.pop(0) for _ in range(PER_TILE)] for kt in range(KT)]
        LAST_A = max(u for u in range(NMX) if MX[u][0] == "A")
        PIECES = 8
        NQ = HPG * 4
        O_BANKS = [0, 1, 2, 3, 5, 6]
        PER_LAYER = {
            "ctx_in": 16, "w_in": 48, "wo_zero": 1, "wo_in": 64, "b_in": 64, "bq_set": 1,
            "var_set": 1, "rstd_set": 1, "xn_set": TT,
            "k_full": 2 * QC, "v_full": KT, "xt_full": 2 * QC, "q_full": 2 * QC,
            "k_done": 2 * QC, "v_done": KT, "xt_done": 2 * QC, "q_done": 2 * QC,
            "k_split": 2 * QC, "q_split": 2 * QC, "k_out0": 16 * QC, "k_out1": 16 * QC, "q_out0": 16 * QC, "q_out1": 16 * QC,
            "q_first": 2 * QC, "k_ones": 1, "q_ones": 1, "fill_set": 1, "fill_in": 48, "qk_in": 16 * 96, "vg_zero": 2, "v_ones": 1, "vg_set": NIT,
            "mx_full": NIT * NMX, "mx_done": NIT * NMX, "negm_set": NIT, "m_full": NIT, "mc": 4 * NIT, "m_split": NIT,
            "m_out": 16 * NIT, "m_in": 16 * NIT, "sc_full": NIT * 2 * KT, "p_set": NIT * 2 * KT,
            "pv_done": NIT * KT, "ot_set": NIT, "sum_full": NIT, "sum_out": NIT, "inv_set": NIT, "on_set": NIT,
            "x_re": 16, "bo_add": 1, "o_full": TT, "x_add": TT}

        def attention_loads(sp, pre):
            sp.dma_start(ctxT, w["ctxT"].rearrange("(k p) s -> p k s", p=P)).then_inc(sem("ctx_in"), 16)
            for i, n in enumerate(("Wk", "Wv", "Wq")):
                sp.dma_start(wqkv[:, i, :, :], w[pre + n].rearrange("(k p) o -> p k o", p=P)).then_inc(sem("w_in"), 16)

        def moe_sync(sp):
            sp.wait_ge(sem("x_add"), TT)
            sp.dma_start(dr_x.rearrange("(t p) d -> p t d", p=P), x_sb[:, :, :]).then_inc(sem("x_saved"), 16)
            sp.dma_start(r1w, w["r1T"].rearrange("(k p) j -> p k j", p=P)).then_inc(sem("r_in"), 16)
            sp.dma_start(r1s, w["r1sT"]).then_inc(sem("r_in"), 16)
            sp.dma_start(r2w, w["r2T"]).then_inc(sem("r_in"), 16)
            sp.dma_start(r1b, w["L0_ffn_r1_b"].rearrange("(p o) -> p o", o=1)).then_inc(sem("r_in"), 16)

            def load(e, s, g, first):
                if not first:
                    sp.wait_ge(sem("dn_done"), e - SLOTS + (2 if s % 2 == 0 else 1))
                sp.dma_start(up_w[s], w["upT"][bass.ds(e, 1), :, :].rearrange("e (k p) j -> p (e k) j", p=P)).then_inc(sem(f"up_in{s}"), 16)
                sp.dma_start(dn_w[s], w["dnT"][bass.ds(e, 1), :, :].rearrange("e (k p) o -> p (e k) o", p=P)).then_inc(sem(f"dn_in{s}"), 16)
                if s % 2 == 0:
                    b = s // 2
                    sp.dma_start(aup_w[b], w["aupT"][bass.ds(g, 1), :, :].rearrange("e (k p) j -> p (e k) j", p=P)).then_inc(sem(f"a_in{b}"), 16)
                    sp.dma_start(adn_w[b], w["adnT"][bass.ds(g, 1), :, :].rearrange("e p o -> p (e o)")).then_inc(sem(f"a_in{b}"), 16)

            sp.wait_ge(sem("x_saved"), 16)
            sp.wait_ge(sem("xn_set_m"), TT)
            for s in range(SLOTS):
                load(s, s, s // 2, True)
            sp.wait_ge(sem("den_set"), 1)
            tab_v = dr_tab.rearrange("(t p) d -> p t d", p=P)
            sp.dma_start(tab_v[:, :, 0:D], xn).then_inc(sem("tab_out"), 16)
            sp.dma_start(tab_v[:, :, D:D + 1], den.rearrange("p (t o) -> p t o", o=1),
                         allow_slow_non_contiguous=True).then_inc(sem("tab_out"), 16)
            sp.wait_ge(sem("differ_set"), 1)
            attention_loads(sp, "L1_xattn_")
            with sp.Fori(1, E // SLOTS) as r:
                for s in range(SLOTS):
                    load(r * SLOTS + s, s, r * (SLOTS // 2) + s // 2, False)
            for b in range(2):
                sp.wait_ge(sem(f"sc_done{b}"), 16 * E // 2)
            sp.dma_start(x_sb[:, :, :], dr_x.rearrange("(t p) d -> p t d", p=P)).then_inc(sem("x_back"), 16)

        def final_sync(sp):
            sp.wait_ge(sem("x_add"), 2 * TT)
            sp.dma_start(fkb, a["fk"].rearrange("(k p) o -> p k o", p=P)).then_inc(sem("f_in"), 16)
            sp.dma_start(fsc[:, 0:1], a["s_in"].partition_broadcast(P)).then_inc(sem("f_in"), 16)
            sp.dma_start(fsc[:, 1:2], a["s_k"].partition_broadcast(P)).then_inc(sem("f_in"), 16)
            sp.dma_start(fbb, a["fbias"].partition_broadcast(P)).then_inc(sem("f_in"), 16)


        @block.sync
        def _(sp):
            for L in range(2):
                pre = f"L{L}_xattn_"
                was = lambda n, L=L: L * PER_LAYER[n]
                if L == 0:
                    attention_loads(sp, pre)
                if L == 0:
                    x_v = w["x"].rearrange("a (t p) d -> p (a t) d", p=P)
                    for c in range(4):
                        sp.dma_start(x_sb[:, 4 * c:4 * c + 4, :], x_v[:, 4 * c:4 * c + 4, :]).then_inc(sem("x_in"), 16)
                else:
                    sp.wait_ge(sem("key_out"), 16)
                    sp.dma_start(keepB[96:P, :], dr_key[0:S2].partition_broadcast(P - 96)).then_inc(sem("left_out_in"), 16)
                sp.wait_ge(sem("wo_zero"), was("wo_zero") + 1)
                for i in range(HPG):
                    sp.dma_start(wo[32 * i:32 * i + HD, :, :],
                                 w[pre + "Wo"].rearrange("(g i d) o -> i d g o", g=HG, i=HPG)[i]).then_inc(sem("wo_in"), 16)
                def back(kind, i):
                    m, c = i // QC, i % QC
                    c0, cn = chunk(c) if kind == "k" else (c * CH, CH)
                    sp.wait_ge(sem(f"{kind}_out{i % 2}"), was(f"{kind}_out{i % 2}") + 16 * (i // 2 + 1))
                    for j in range(6):
                        if kind == "k":
                            to, parts = Kp, dr_k[K_PART[j]]
                        else:
                            to, parts = Qp, dr_q[Q_PART[j]]
                        sp.dma_start(to[HD * j:HD * (j + 1), m * 8:(m + 1) * 8, c0:c0 + cn],
                                     parts[m * P:(m + 1) * P, c0:c0 + cn].rearrange("(h d) t -> d h t", d=HD)).then_inc(sem("qk_in"), 16)

                for kind, dst in (("k", dr_k), ("q", dr_q)):
                    if kind == "q":
                        sp.wait_ge(sem("k_ones"), was("k_ones") + 1)
                        sp.wait_ge(sem("fill_set"), was("fill_set") + 1)
                        for part in range(3):
                            sp.dma_start(Kp[96 + part:97 + part, :, :],
                                         fillr[96 + part:97 + part, :].rearrange("p (o s) -> p o s", o=1).to_broadcast([1, NH, S2]))\
                                .then_inc(sem("fill_in"), 16)
                        sp.wait_ge(sem("xn_set"), was("xn_set") + TT)
                    for i in range(2 * QC):
                        m, c = i // QC, i % QC
                        c0, cn = chunk(c) if kind == "k" else (c * CH, CH)
                        sp.wait_ge(sem(kind + "_split"), was(kind + "_split") + i + 1)
                        sp.dma_start(dst[:, m * P:(m + 1) * P, c0:c0 + cn].rearrange("i p t -> p i t"),
                                     stg_p[i % 2][:, :, 0:cn]).then_inc(sem(f"{kind}_out{i % 2}"), 16)
                        if i:
                            back(kind, i - 1)
                    back(kind, 2 * QC - 1)

                def m_rows(n):
                    sp.wait_ge(sem("m_split"), was("m_split") + n + 1)
                    sp.dma_start(dr_m[bass.ds(n, 1), :, :].rearrange("n i (u c) -> u (n i) c", c=P),
                                 mparts[:, :, :]).then_inc(sem("m_out"), 16)
                    sp.wait_ge(sem("m_out"), was("m_out") + 16 * n + 16)
                    sp.dma_start(Qp[PASS1_ROWS:PASS2_ROWS, bass.ds((n // QC) * HPG, HPG), bass.ds((n % QC) * CH, CH)],
                                 dr_m[bass.ds(n, 1), :, :].rearrange("n i (h c) -> (n i) h c", c=CH)).then_inc(sem("m_in"), 16)

                with sp.Fori(0, NIT // 2) as n:
                    m_rows(n)
                sp.wait_ge(sem("sc_full"), was("sc_full") + QC * 2 * KT)
                sp.dma_start(x_sb, w["x"].rearrange("a (t p) d -> p (a t) d", p=P) if L == 0 else
                             dr_x.rearrange("(t p) d -> p t d", p=P)).then_inc(sem("x_re"), 16)
                with sp.Fori(NIT // 2, NIT) as n:
                    m_rows(n)
                if L == 0:
                    moe_sync(sp)
            final_sync(sp)
            sp.wait_ge(sem("x_out"), TT)
            sp.dma_start(a["out"].rearrange("a (t p) d -> p (a t) d", p=P), x_sb[:, :, :]).then_inc(sem("out_done"), 16)
            sp.wait_ge(sem("out_done"), 16)

        def moe_pool(pool):
            pool.wait_ge(sem("x_add"), TT)
            nc.gpsimd.iota(iot, pattern=[[0, TT], [1, E]], base=0, channel_multiplier=0,
                           allow_small_or_imprecise_dtypes=True).then_inc(sem("iota_set"), 1)
            pool.wait_ge(sem("var_set_m"), 1)
            nc.gpsimd.tensor_tensor(lnt[6], lnt[5], expo[:, 0:1].to_broadcast([P, 16]), ALU.pow).then_inc(sem("rstd_set_m"), 1)
            pool.wait_ge(sem("var2_set"), 2)
            nc.gpsimd.tensor_tensor(st[:, :, 1], lnt[7], expo[:, 1:2].to_broadcast([P, 16]), ALU.pow).then_inc(sem("root_set"), 1)
            nc.gpsimd.tensor_tensor(st[:, :, 4], lnt[8], expo[:, 1:2].to_broadcast([P, 16]), ALU.pow).then_inc(sem("root_set"), 1)
            pool.wait_ge(sem("tab_out"), 32)
            pool.wait_ge(sem("idx_set"), 2)
            pool.wait_ge(sem("x_saved"), 16)

            def gather(e):
                if e >= 4:
                    pool.wait_ge(sem("w_set"), e - 3)
                    pool.wait_ge(sem("xe_t"), e - 3)
                pool.indirect_dma_start(xe[e % 4], None, dr_tab,
                                        bass.IndirectOffsetOnAxis(ap=idxT[:, e:e + 1], axis=0)).then_inc(sem(f"xe_in{e % 4}"), 16)

            for e in range(4):
                gather(e)
            for e in range(E):
                pool.wait_ge(sem("ye_set"), e + 1)
                if e:
                    pool.wait_ge(sem(f"sc_done{(e - 1) % 2}"), 16 * ((e + 1) // 2))
                pool.indirect_dma_start(dr_x, bass.IndirectOffsetOnAxis(ap=idxT[:, e:e + 1], axis=0), ye[e % 2], None,
                                        compute_op=ALU.add).then_inc(sem(f"sc_done{e % 2}"), 16)
                if e + 4 < E:
                    gather(e + 4)

        def final_pool(pool):
            pool.wait_ge(sem("x_add"), 2 * TT)
            nc.gpsimd.tensor_copy(fidb, ident[:, :]).then_inc(sem("fidb_set"), 1)
            pool.wait_ge(sem("var_setf"), 1)
            nc.gpsimd.tensor_tensor(lnt[6], lnt[5], expo[:, 0:1].to_broadcast([P, 16]), ALU.pow).then_inc(sem("rstd_setf"), 1)

        def mask_tile(pool, kt, kn):
            wait(pool, sem("mm_tree"), kt * MM_LEVELS)
            pool.nop(nofuse=True)
            pool.dma_start(mchk[0:kn, :], w["mask1T"][bass.ds(kt * P, kn), :]).then_inc(sem("mchk_in"), 16)
            pool.wait_ge(sem("mchk_in"), kt * 16 + 16)
            half, src = T, mchk
            for level in range(MM_LEVELS):
                half //= 2
                if level:
                    pool.wait_ge(sem("mm_tree"), kt * MM_LEVELS + level)
                out = mchk[0:kn, 0:half] if level == 0 else mtree[0:kn, 0:half] if half > 1 else mm_key[0:kn, bass.ds(kt, 1)]
                nc.gpsimd.tensor_tensor(out, src[0:kn, 0:half], src[0:kn, half:2 * half], ALU.add).then_inc(sem("mm_tree"), 1)
                src = mchk if level == 0 else mtree

        def mask_verdict(pool):
            pool.wait_ge(sem("mm_tree"), KT * MM_LEVELS)
            nc.gpsimd.tensor_scalar(mm_flag[:, 0, :], mm_key[:, :], float(T), None, ALU.is_equal).then_inc(sem("mm_step"), 1)
            pool.wait_ge(sem("mm_step"), 1)
            nc.gpsimd.tensor_scalar(mm_key[:, :], mm_key[:, :], 0.0, None, ALU.is_equal).then_inc(sem("mm_step"), 1)
            pool.wait_ge(sem("mm_step"), 2)
            nc.gpsimd.tensor_tensor(mm_key[:, :], mm_key[:, :], mm_flag[:, 0, :], ALU.add).then_inc(sem("mm_step"), 1)
            pool.wait_ge(sem("mm_step"), 3)
            pool.dma_start(dr_key.rearrange("(t p) -> p t", p=P), mm_flag[:, 0, :],
                           allow_slow_non_contiguous=True).then_inc(sem("key_out"), 16)
            nc.gpsimd.tensor_scalar(mm_key[:, :], mm_key[:, :], -1.0, 1.0, ALU.mult, ALU.add).then_inc(sem("mm_step"), 1)
            pool.wait_ge(sem("mm_step"), 4)
            nc.gpsimd.tensor_reduce(mm_any[0:1, :], mm_key[:, :], AX.XYZWC, ALU.max).then_inc(sem("mm_step"), 1)
            pool.wait_ge(sem("mm_step"), 5)
            nc.gpsimd.tensor_copy(differ[0:1, :], mm_any[0:1, :]).then_inc(sem("differ_set"), 1)

        def mask_unit(pool, n, u):
            what, i, q = MX[u]
            rows = w["mask1"].rearrange("a b q s -> (a b q) s")
            if what == "A":
                if u:
                    last = max(v for v in range(u) if MX[v][0] == "B")
                    pool.wait_ge(sem("mx_full"), PER_LAYER["mx_full"] + n * NMX + last + 1)
                else:
                    pool.wait_ge(sem("mx_full"), PER_LAYER["mx_full"] + n * NMX)
                pool.nop(nofuse=True)
                pool.dma_start(mA, rows[bass.ds((n % QC) * CH + q * P, P), 0:3 * CH]).then_inc(sem("mA_in"), 16)
            elif what == "L" and i == 0:
                pool.wait_ge(sem("mx_full"), PER_LAYER["mx_full"] + n * NMX)
                pool.nop(nofuse=True)
                for qq in range(4):
                    pool.dma_start(mL[:, qq, :], rows[bass.ds((n % QC) * CH + qq * P, P), 3 * CH:S2]).then_inc(sem("mL_in"), 16)

        def mask_loads(pool, n, nxt, nxt2, normalise=None):
            for kt in range(KT):
                kn = P if kt < KT - 1 else KLAST
                pool.wait_ge(sem("sc_full"), PER_LAYER["sc_full"] + n * 2 * KT + max(0, 2 * kt - 2))
                pool.nop(nofuse=True)
                pool.dma_start(mT[kt % 2][0:kn, :], w["mask1T"][kt * P:kt * P + kn, bass.ds((n % QC) * CH, CH)])\
                    .then_inc(sem(f"mT_in{kt % 2}"), 16)
                for ahead, u in MX_AT[kt]:
                    if ahead == 1 and nxt:
                        mask_unit(pool, n + 1, u)
                    if ahead == 2 and nxt2:
                        mask_unit(pool, n + 2, u)
                if kt == M_AT - 2 and normalise:
                    normalise(n - 2)

        @block.gpsimd
        def _(pool):
            nc.gpsimd.memset(ident[:, :], 0.0).then_inc(sem("const"), 1)
            nc.gpsimd.memset(sel[:, :], 0.0).then_inc(sem("const"), 1)
            nc.gpsimd.memset(fillc[:, :], 0.0).then_inc(sem("const"), 1)
            nc.gpsimd.memset(expo[:, 0:1], -0.5).then_inc(sem("const"), 1)
            nc.gpsimd.memset(expo[:, 1:2], 0.5).then_inc(sem("const"), 1)
            nc.gpsimd.memset(tiny[:, :], 1e-30).then_inc(sem("const"), 1)
            pool.wait_ge(sem("const"), 6)
            nc.gpsimd.affine_select(out=ident[:, :], in_=ident[:, :], compare_op=ALU.not_equal, fill=1.0, base=0,
                                    pattern=[[-1, P]], channel_multiplier=1).then_inc(sem("const"), 1)
            nc.gpsimd.affine_select(out=sel[:, :].rearrange("p (i c) -> p i c", c=32), in_=sel[:, :].rearrange("p (i c) -> p i c", c=32),
                                    compare_op=ALU.not_equal, fill=1.0, base=-HD,
                                    pattern=[[-32, HPG], [0, 32]], channel_multiplier=1).then_inc(sem("const"), 1)
            fills = 0
            for L, parts in enumerate((MASK_FILL_PARTS, (NEG_HUGE,))):
                for i, c in enumerate(parts):
                    nc.gpsimd.affine_select(out=fillc[:, L:L + 1], in_=fillc[:, L:L + 1], compare_op=ALU.not_equal,
                                            fill=c, base=-(96 + i), pattern=[[0, 1]], channel_multiplier=1)\
                        .then_inc(sem("fillc"), 1)
                    fills += 1
                    pool.wait_ge(sem("fillc"), fills)
            pool.wait_ge(sem("const"), 8)
            nc.gpsimd.tensor_scalar(neg_id[:, :], ident[:, :], NEG_HUGE, None, ALU.mult).then_inc(sem("neg_id_set"), 1)
            for L in range(2):
                pre = f"L{L}_xattn_"
                was = lambda n, L=L: L * PER_LAYER[n]
                if L == 0:
                    pool.dma_start(keepU, w["mask0"].rearrange("b s -> (b s)").partition_broadcast(P)).then_inc(sem("keep_in"), 16)
                nc.gpsimd.memset(wo[:, :, :], 0.0).then_inc(sem("wo_zero"), 1)
                pool.dma_start(bqk[:, 0, :], w[pre + "bq"].rearrange("(m p) -> p m", p=P), allow_slow_non_contiguous=True).then_inc(sem("b_in"), 16)
                pool.dma_start(bqk[:, 1, :], w[pre + "bk"].rearrange("(m p) -> p m", p=P), allow_slow_non_contiguous=True).then_inc(sem("b_in"), 16)
                pool.dma_start(bvB[:, :], w[pre + "bv"].partition_broadcast(P)).then_inc(sem("b_in"), 16)
                pool.dma_start(boB[:, :], w[pre + "bo"].partition_broadcast(P)).then_inc(sem("b_in"), 16)
                pool.wait_ge(sem("wo_zero"), was("wo_zero") + 1)
                if L == 1:
                    pool.wait_ge(sem("x_back"), 16)
                nc.gpsimd.memset(Kp_flat[96:P, :].bitcast(F32), ONES_BF16_PAIR).then_inc(sem("k_ones"), 1)
                pool.wait_ge(sem("k_ones"), was("k_ones") + 1)
                pool.wait_ge(sem("var_set"), was("var_set") + 1)
                nc.gpsimd.tensor_tensor(lnt[6], lnt[5], expo[:, 0:1].to_broadcast([P, TT]), ALU.pow).then_inc(sem("rstd_set"), 1)
                pool.wait_ge(sem("xn_set"), was("xn_set") + TT)
                nc.gpsimd.memset(QKf[96:P, :], ONES_BF16_PAIR).then_inc(sem("q_ones"), 1)
                pool.wait_ge(sem("q_ones"), was("q_ones") + 1)
                pool.wait_ge(sem("xt_full"), was("xt_full") + 2 * QC)
                for b in range(2):
                    nc.gpsimd.memset(Vg[b], 0.0).then_inc(sem("vg_zero"), 1)
                pool.wait_ge(sem("vg_zero"), was("vg_zero") + 2)
                pool.wait_ge(sem("fill_in"), was("fill_in") + 48)
                nc.gpsimd.memset(Vp[:, :, :, :], 1.0).then_inc(sem("v_ones"), 1)
                pool.wait_ge(sem("v_done"), was("v_done") + KT)
                pool.wait_ge(sem("vg_zero"), was("vg_zero") + 2)

                def v_copy(n, b):
                    wait(pool, sem("pv_done"), was("pv_done") + n * KT - KT)
                    nc.gpsimd.tensor_copy(Vg[b][:, :, 0:HD + 1],
                                          Vp[:, bass.ds(n // QC, 1), :, :].rearrange("p a u c -> p (a u) c")).then_inc(sem("vg_set"), 1)

                def normalise(n):
                    pool.wait_ge(sem("inv_set"), was("inv_set") + n + 1)
                    out = OT[:, bass.ds(n, 1), :].rearrange("p a c -> p (a c)")
                    nc.gpsimd.tensor_tensor(out, out, rsum, ALU.mult).then_inc(sem("on_set"), 1)

                v_copy(0, 0)
                v_copy(1, 1)
                if L == 0:
                    assert KT == NIT - 3
                    nc.gpsimd.memset(mm_key[:, :], float(T)).then_inc(sem("mm_init"), 1)
                    pool.wait_ge(sem("mm_init"), 1)
                    pool.wait_ge(sem("v_full"), KT)
                    for n in (2, 3):
                        v_copy(n, n % 2)
                        normalise(n - 2)
                        mask_tile(pool, n - 2, P)
                    with pool.Fori(2, NIT // 2 - 1) as pair:
                        for b in range(2):
                            v_copy(2 * pair + b, b)
                            normalise(2 * pair + b - 2)
                            mask_tile(pool, 2 * pair + b - 2, P)
                    v_copy(NIT - 2, 0)
                    normalise(NIT - 4)
                    mask_tile(pool, KT - 1, KLAST)
                    mask_verdict(pool)
                    v_copy(NIT - 1, 1)
                    normalise(NIT - 3)
                else:
                    pool.wait_ge(sem("v_full"), 2 * PER_LAYER["v_full"])
                    pool.wait_ge(sem("differ_set"), 1)
                    whole = pool.value_load(differ[0:1, 0:1], min_val=0, max_val=1)
                    with pool.If(whole == 1):
                        for u in range(NMX):
                            mask_unit(pool, 0, u)
                        for u in range(AHEAD2):
                            mask_unit(pool, 1, u)
                        for n in range(2):
                            mask_loads(pool, n, True, True)
                        with pool.Fori(1, NIT // 2 - 1) as pair:
                            for b in range(2):
                                v_copy(2 * pair + b, b)
                                mask_loads(pool, 2 * pair + b, True, True, normalise)
                        v_copy(NIT - 2, 0)
                        mask_loads(pool, NIT - 2, True, False, normalise)
                        v_copy(NIT - 1, 1)
                        mask_loads(pool, NIT - 1, False, False, normalise)
                    with pool.Else():
                        with pool.Fori(1, NIT // 2) as pair:
                            for b in range(2):
                                v_copy(2 * pair + b, b)
                                normalise(2 * pair + b - 2)
                pool.wait_ge(sem("x_re"), was("x_re") + 16)
                nc.gpsimd.tensor_tensor(x_sb, x_sb, boB[:, :].rearrange("p (o d) -> p o d", o=1).to_broadcast([P, TT, D]), ALU.add)\
                    .then_inc(sem("bo_add"), 1)
                normalise(NIT - 2)
                normalise(NIT - 1)
                if L == 0:
                    moe_pool(pool)
            final_pool(pool)

        def moe_pe(pe):
            pe.wait_ge(sem("x_add"), TT)
            for i in range(2 * QC):
                h, c = i % DH, i // DH
                pe.wait_ge(sem("xn_set_m"), 4 * c + 4)
                for j in range(4):
                    mm = nc.tensor.transpose(ps[:, i, j * P:(j + 1) * P], xn[:, 4 * c + j, h * P:(h + 1) * P], ident[:, :])
                mm.then_inc(sem("xt_full_m"), 1)
            pe.wait_ge(sem("xt_done_m"), 2 * QC)
            pe.wait_ge(sem("st_set"), 3)
            pe.wait_ge(sem("root_set"), 2)
            for c in range(QC):
                for j in range(4):
                    mm = nc.tensor.transpose(ps[0:6, c, j * P:(j + 1) * P], st[:, 4 * c + j, :], ident[:, :])
                mm.then_inc(sem("stt_full"), 1)
            pe.wait_ge(sem("r_in"), 64)
            for c in range(QC):
                pe.wait_ge(sem("stt_done"), c + 1)
                for k in range(DH):
                    nc.tensor.matmul(ps[:, 4 + c, :], r1w[:, k, :], xfT[:, k, c * CH:(c + 1) * CH], start=(k == 0), stop=False)
                nc.tensor.matmul(ps[:, 4 + c, :], r1s, stT[:, c * CH:(c + 1) * CH], start=False, stop=True).then_inc(sem("rh_full"), 1)
            for t in range(TT):
                pe.wait_ge(sem("rh_set"), t // 4 + 1)
                mm = nc.tensor.matmul(ps[:, 0, t * E:(t + 1) * E], hT[:, t * P:(t + 1) * P], r2w, start=True, stop=True)
            mm.then_inc(sem("lg_full"), 1)
            pe.wait_ge(sem("score_set"), 1)
            for t in range(TT):
                mm = nc.tensor.transpose(ps[0:E, 1 + t // 4, (t % 4) * P:(t % 4 + 1) * P], prb[:, t, :], ident[:, :])
            mm.then_inc(sem("sct_full"), 1)
            pe.wait_ge(sem("top_set"), 1)
            nc.tensor.transpose(ps[0:CAP, 5, 0:E], vals, ident[0:E, 0:E])
            nc.tensor.transpose(ps[0:CAP, 5, E:2 * E], idxf, ident[0:E, 0:E]).then_inc(sem("topT_full"), 1)

            def rows_transpose(r, s):
                e = r * SLOTS + s
                pe.wait_ge(sem(f"xe_in{s}"), 16 * r + 16)
                wait(pe, sem("xeT_set"), e)
                for k in range(DH):
                    mm = nc.tensor.transpose(ps[:, 5, k * CAP:(k + 1) * CAP], xe[s][:, k * P:(k + 1) * P], ident[0:CAP, 0:CAP])
                mm.then_inc(sem("xe_t"), 1)

            def gate_up(r, s):
                b = s % 2
                pe.wait_ge(sem("xeT_set"), r * SLOTS + s + 1)
                pe.wait_ge(sem(f"up_in{s}"), 16 * r + 16)
                wait(pe, sem(f"hh_set{b}"), r * 2 + s // 2)
                for j, bank in ((0, b), (1, 2 + b)):
                    for k in range(DH):
                        nc.tensor.matmul(ps[0:CAP, bank, :], xeT[b][:, k, :], up_w[s][:, k, j * CH:(j + 1) * CH],
                                         start=(k == 0), stop=(k == DH - 1))

            def adapter(r, s):
                b = s % 2
                pe.wait_ge(sem(f"a_in{s // 2}"), 32 * r + 32)
                wait(pe, sem(f"hh_set{1 - b}"), r * 2 + (s + 1) // 2)
                for k in range(DH):
                    mm = nc.tensor.matmul(ps[0:CAP, 4, 0:2 * A_INTER], xeT[b][:, k, :], aup_w[s // 2][:, k, :],
                                          start=(k == 0), stop=(k == DH - 1))
                mm.then_inc(sem("up_full"), 1)

            def hidden_transpose(r, s):
                b = s % 2
                pe.wait_ge(sem(f"hh_set{b}"), r * 2 + s // 2 + 1)
                wait(pe, sem("hhT_set"), r * SLOTS + s)
                for k in range(5):
                    mm = nc.tensor.transpose(ps[:, 6, k * CAP:(k + 1) * CAP], hh[b][:, k * P:(k + 1) * P], ident[0:CAP, 0:CAP])
                mm.then_inc(sem("hhT_full"), 1)

            def down(r, s):
                b = s % 2
                e = r * SLOTS + s
                pe.wait_ge(sem("hhT_set"), e + 1)
                pe.wait_ge(sem(f"dn_in{s}"), 16 * r + 16)
                wait(pe, sem("ye_set"), e)
                for k in range(5):
                    mm = nc.tensor.matmul(ps[0:CAP, 7, 0:D], hhT[b][:, k, :], dn_w[s][:, k, :] if k < 4 else adn_w[s // 2],
                                          start=(k == 0), stop=(k == 4))
                mm.then_inc(sem("dn_done"), 1)

            def round_(r, last):
                for s in range(SLOTS):
                    one, two = (r + (s + 1) // SLOTS, (s + 1) % SLOTS), (r + (s + 2) // SLOTS, (s + 2) % SLOTS)
                    if not (last and s + 1 == SLOTS):
                        gate_up(*one)
                    hidden_transpose(r, s)
                    if not (last and s + 1 == SLOTS):
                        adapter(*one)
                    if not (last and s + 2 >= SLOTS):
                        rows_transpose(*two)
                    down(r, s)

            pe.wait_ge(sem("idx_set"), 2)
            rows_transpose(0, 0)
            rows_transpose(0, 1)
            gate_up(0, 0)
            adapter(0, 0)
            round_(0, False)
            with pe.Fori(1, E // SLOTS - 1) as r:
                round_(r, False)
            round_(E // SLOTS - 1, True)

        def final_pe(pe):
            pe.wait_ge(sem("fidb_set"), 1)
            pe.wait_ge(sem("x_add"), 2 * TT)
            for c in range(QC):
                pe.wait_ge(sem("fx_set"), c + 1)
                bank = ps[:, c, :].bitcast(BF16)
                for k in range(DH):
                    for j in range(4):
                        mm = nc.tensor.transpose(bank[:, k * CH + j * P:k * CH + (j + 1) * P],
                                                 fxb[:, (4 * c + j) * D + k * P:(4 * c + j) * D + (k + 1) * P], fidb)
                mm.then_inc(sem("fxT_full"), 1)
            pe.wait_ge(sem("fk_set"), 1)
            for t in range(TT):
                pe.wait_ge(sem("fxT_set"), t // 4 + 1)
                if t >= 4:
                    pe.wait_ge(sem("x_out"), t - 3)
                for k in range(DH):
                    mm = nc.tensor.matmul(ps[:, 4 + t % 4, 0:D], fxT[:, k, t * P:(t + 1) * P], fkq[:, k, :],
                                          start=(k == 0), stop=(k == DH - 1))
                mm.then_inc(sem("y_full"), 1)

        @block.tensor
        def _(pe):
            pe.wait_ge(sem("const"), 8)
            for L in range(2):
                was = lambda n, L=L: L * PER_LAYER[n]
                pe.wait_ge(sem("ctx_in"), was("ctx_in") + 16)
                if L == 1:
                    pe.wait_ge(sem("ye_set"), E)
                pe.wait_ge(sem("w_in"), was("w_in") + 48)
                for pos, (kind, i) in enumerate(prep_units()):
                    bank = pos % 8
                    if before(pos):
                        k2, i2 = before(pos)
                        pe.wait_ge(sem(k2 + "_done"), was(k2 + "_done") + i2 + 1)
                        if k2 == "q":
                            pe.wait_ge(sem("q_first"), was("q_first") + i2 + 1)
                        if k2 == "k" and L == 1:
                            pe.wait_ge(sem("k_first"), i2 + 1)
                    if kind == "k":
                        m, c = i // QC, i % QC
                        c0, cn = chunk(c)
                        for k in range(DH):
                            mm = nc.tensor.matmul(ps[:, bank, 0:cn], wqkv[:, 0, k, m * P:(m + 1) * P],
                                                  ctxT[:, k, c0:c0 + cn], start=(k == 0), stop=(k == DH - 1))
                    elif kind == "v":
                        kn = P if i < KT - 1 else KLAST
                        for k in range(DH):
                            mm = nc.tensor.matmul(ps[0:kn, bank, 0:D], ctxT[:, k, i * P:i * P + kn],
                                                  wqkv[:, 1, k, :], start=(k == 0), stop=(k == DH - 1))
                    elif kind == "xt":
                        h, c = i % DH, i // DH
                        pe.wait_ge(sem("xn_set"), was("xn_set") + 4 * c + 4)
                        for j in range(4):
                            mm = nc.tensor.transpose(ps[:, bank, j * P:(j + 1) * P], xn[:, 4 * c + j, h * P:(h + 1) * P], ident[:, :])
                    else:
                        m, c = i // QC, i % QC
                        pe.wait_ge(sem("xt_done"), was("xt_done") + (DH * (c + 1) if m == 0 else DH * QC))
                        for k in range(DH):
                            mm = nc.tensor.matmul(ps[:, bank, :], wqkv[:, 2, k, m * P:(m + 1) * P],
                                                  xnT[:, k, c * CH:(c + 1) * CH], start=(k == 0), stop=(k == DH - 1))
                    mm.then_inc(sem(kind + "_full"), 1)
                pe.wait_ge(sem("q_first"), was("q_first") + 2 * QC)
                pe.wait_ge(sem("v_done"), was("v_done") + KT)
                pe.wait_ge(sem("fill_in"), was("fill_in") + 48)
                pe.wait_ge(sem("qk_in"), was("qk_in") + 16 * 96)
                pe.wait_ge(sem("q_ones"), was("q_ones") + 1)

                def scores(out, lhsT, rhs, mask, kn, masked):
                    mm = nc.tensor.matmul(out, lhsT, rhs, start=True, stop=not masked)
                    if masked:
                        mm = nc.tensor.matmul(out, neg_id[0:kn, 0:kn], mask, start=False, stop=True)
                    return mm

                def mx_unit(n, u, masked):
                    what, i, q = MX[u]
                    g, qc = n // QC, n % QC
                    h = g * HPG + i
                    prev = [v for v in range(u) if (MX[v][0] == "A") == (what == "A")]
                    if prev:
                        pe.wait_ge(sem("mx_done"), was("mx_done") + n * NMX + prev[-1] + 1)
                    else:
                        wait(pe, sem("mx_done"), was("mx_done") + n * NMX)
                        if what == "A" and not (isinstance(n, int) and n < 3):
                            pe.wait_ge(sem("sum_out"), was("sum_out") + n - 2)
                        if what == "B" and not (isinstance(n, int) and n == 0):
                            pe.wait_ge(sem("mc"), was("mc") + n * 4 - 3)
                    Kh = lambda c0, cn: Kp[0:PASS1_ROWS, bass.ds(h, 1), c0:c0 + cn].rearrange("p a b -> p (a b)")
                    Qh = lambda qq: Qp[0:PASS1_ROWS, bass.ds(h, 1), bass.ds(qc * CH + qq * P, P)].rearrange("p a b -> p (a b)")
                    if what == "A":
                        if masked:
                            pe.wait_ge(sem("mA_in"), 16 * (n * NQ + i * 4 + q + 1))
                        for j in range(2):
                            mm = scores(ps[:, 4 + j, :], Qh(q), Kh(j * CH, CH), mA[:, j * CH:(j + 1) * CH], P, masked)
                    elif what == "B":
                        mm = scores(ps[:, 6, :], Qh(q), Kh(2 * CH, CH), mA[:, 2 * CH:3 * CH], P, masked)
                    else:
                        if masked:
                            pe.wait_ge(sem("mL_in"), 64 * (n + 1))
                        for qq in range(4):
                            mm = scores(ps[:, 6, qq * KLAST:(qq + 1) * KLAST], Qh(qq), Kh(3 * CH, KLAST), mL[:, qq, :], P, masked)
                    mm.then_inc(sem("mx_full"), 1)

                def m_transpose(n):
                    pe.wait_ge(sem("negm_set"), was("negm_set") + n + 1)
                    nc.tensor.transpose(ps[0:16, 6, 0:P], negm[:, :], ident[:, :]).then_inc(sem("m_full"), 1)

                def pv(n, b, kt):
                    kn = P if kt < KT - 1 else KLAST
                    pe.wait_ge(sem("p_set"), was("p_set") + n * 2 * KT + 2 * kt + 2)
                    if kt == 0:
                        pe.wait_ge(sem("vg_set"), was("vg_set") + n + 1)
                        wait(pe, sem("ot_set"), was("ot_set") + n)
                    for i in range(HPG):
                        mm = nc.tensor.matmul(ps[32 * i:32 * i + 32, 7, :], Vg[b][0:kn, kt * HPG + i, :],
                                              Pt[(2 * (KT * b + kt) + i // 2) % 4][0:kn, (i % 2) * CH:(i % 2 + 1) * CH],
                                              start=(kt == 0), stop=(kt == KT - 1))
                    mm.then_inc(sem("pv_done"), 1)

                def sum_unit(n, free):
                    pe.wait_ge(sem("ot_set"), was("ot_set") + n + 1)
                    pe.wait_ge(sem("mx_done"), was("mx_done") + free)
                    nc.tensor.matmul(ps[:, 4, :], sel[:, :], OT[:, bass.ds(n, 1), :].rearrange("p a c -> p (a c)"),
                                     start=True, stop=True).then_inc(sem("sum_full"), 1)

                def iteration(n, b, nxt, nxt2, masked):
                    g, qc = n // QC, n % QC

                    def maxima(kt, i):
                        for ahead, u in MX_AT[kt][i:i + 1]:
                            if ahead == 1 and nxt:
                                mx_unit(n + 1, u, masked)
                            if ahead == 2 and nxt2:
                                mx_unit(n + 2, u, masked)

                    pe.wait_ge(sem("m_in"), was("m_in") + 16 * n + 16)
                    for kt in range(KT):
                        kn = P if kt < KT - 1 else KLAST
                        if masked:
                            pe.wait_ge(sem(f"mT_in{kt % 2}"), 16 * (n * ((KT + 1 - kt % 2) // 2) + kt // 2 + 1))
                        for half in range(2):
                            v = 2 * kt + half
                            wait(pe, sem("p_set"), was("p_set") + n * 2 * KT + v - 1)
                            for i in (2 * half, 2 * half + 1):
                                h = g * HPG + i
                                mm = scores(ps[0:kn, 2 * (v % 2) + i % 2, :],
                                            Kp[0:PASS2_ROWS, bass.ds(h, 1), kt * P:kt * P + kn].rearrange("p a b -> p (a b)"),
                                            Qp[0:PASS2_ROWS, bass.ds(h, 1), bass.ds(qc * CH, CH)].rearrange("p a b -> p (a b)"),
                                            mT[kt % 2][0:kn, :], kn, masked)
                            mm.then_inc(sem("sc_full"), 1)
                            maxima(kt, half)
                        if kt == M_AT and nxt:
                            m_transpose(n + 1)
                        if kt == M_AT and not (isinstance(n, int) and n == 0):
                            sum_unit(n - 1, (n + 1) * NMX + LAST_A + 1 if nxt else NIT * NMX)
                        if kt:
                            pv(n, b, kt - 1)
                        elif not (isinstance(n, int) and n == 0):
                            pv(n - 1, 1 - b, KT - 1)
                        maxima(kt, 2)

                def iterations(masked):
                    for u in range(NMX):
                        mx_unit(0, u, masked)
                    m_transpose(0)
                    for u in range(AHEAD2):
                        mx_unit(1, u, masked)
                    iteration(0, 0, True, True, masked)
                    iteration(1, 1, True, True, masked)
                    with pe.Fori(1, NIT // 2 - 1) as pair:
                        for b in range(2):
                            iteration(2 * pair + b, b, True, True, masked)
                    iteration(NIT - 2, 0, True, False, masked)
                    iteration(NIT - 1, 1, False, False, masked)
                    pv(NIT - 1, 1, KT - 1)

                if L == 0:
                    iterations(False)
                else:
                    pe.wait_ge(sem("neg_id_set"), 1)
                    pe.wait_ge(sem("differ_set"), 1)
                    whole = pe.value_load(differ[0:1, 0:1], min_val=0, max_val=1)
                    with pe.If(whole == 1):
                        iterations(True)
                    with pe.Else():
                        iterations(False)

                pe.wait_ge(sem("wo_in"), was("wo_in") + 64)
                pe.wait_ge(sem("p_set"), was("p_set") + NIT * 2 * KT)
                for t in range(TT):
                    if t == 2:
                        sum_unit(NIT - 1, NIT * NMX)
                    pe.wait_ge(sem("on_set"), was("on_set") + (HG - 1) * QC + t // 4 + 1)
                    if t >= len(O_BANKS):
                        pe.wait_ge(sem("x_add"), was("x_add") + t - len(O_BANKS) + 1)
                    for g in range(HG):
                        mm = nc.tensor.matmul(ps[:, O_BANKS[t % len(O_BANKS)], 0:D], OT[:, g * QC + t // 4, (t % 4) * P:(t % 4 + 1) * P],
                                              wo[:, g, :], start=(g == 0), stop=(g == HG - 1))
                    mm.then_inc(sem("o_full"), 1)
                if L == 0:
                    moe_pe(pe)
            final_pe(pe)

        def moe_act(act):
            for i in range(2 * QC):
                h, c = i % DH, i // DH
                act.wait_ge(sem("xt_full_m"), i + 1)
                nc.scalar.activation(xfT[:, h, c * CH:(c + 1) * CH], ps[:, i, :], ACT.Copy).then_inc(sem("xt_done_m"), 1)
            act.wait_ge(sem("r_in"), 64)
            for c in range(QC):
                act.wait_ge(sem("rh_full"), c + 1)
                nc.scalar.activation(hT[:, c * CH:(c + 1) * CH], ps[:, 4 + c, :], ACT.Gelu, bias=r1b).then_inc(sem("rh_set"), 1)
            act.wait_ge(sem("lg_sub"), 1)
            nc.scalar.activation(lg.rearrange("p t e -> p (t e)"), lg.rearrange("p t e -> p (t e)"), ACT.Exp).then_inc(sem("lg_exp"), 1)

            def silu(r, s):
                b = s % 2
                e = r * SLOTS + s
                act.wait_ge(sem("up_full"), e + 1)
                wait(act, sem(f"hh_set{b}"), r * 2 + s // 2)
                nc.scalar.activation(sg[b][:, 0:INTER], ps[0:CAP, b, :], ACT.Silu)
                nc.scalar.activation(sg[b][:, INTER:HALL], ps[0:CAP, 4, 0:A_INTER], ACT.Silu).then_inc(sem("silu_set"), 1)

            for s in range(SLOTS):
                silu(0, s)
            with act.Fori(1, E // SLOTS) as r:
                for s in range(SLOTS):
                    silu(r, s)

        def final_act(act):
            for c in range(QC):
                act.wait_ge(sem("fxT_full"), c + 1)
                nc.scalar.activation(fxT[:, :, c * CH:(c + 1) * CH],
                                     ps[:, c, :].bitcast(BF16).rearrange("p (k t) -> p k t", k=2), ACT.Copy).then_inc(sem("fxT_set"), 1)

        @block.scalar
        def _(act):
            act.wait_ge(sem("const"), 8)
            for L in range(2):
                was = lambda n, L=L: L * PER_LAYER[n]
                act.wait_ge(sem("b_in"), was("b_in") + 64)
                if L == 1:
                    act.wait_ge(sem("x_back"), 16)
                nc.scalar.mul(bqk[:, 0, :], bqk[:, 0, :], HD ** -0.5).then_inc(sem("bq_set"), 1)
                act.wait_ge(sem("bq_set"), was("bq_set") + 1)
                for pos, (kind, i) in enumerate(prep_units()):
                    bank = pos % 8
                    if kind == "v":
                        continue
                    act.wait_ge(sem(kind + "_full"), was(kind + "_full") + i + 1)
                    if kind == "xt":
                        h, c = i % DH, i // DH
                        nc.scalar.activation(xnT[:, h, c * CH:(c + 1) * CH], ps[:, bank, :], ACT.Copy).then_inc(sem("xt_done"), 1)
                        continue
                    m, c = i // QC, i % QC
                    cn = chunk(c)[1] if kind == "k" else CH
                    if i >= 2:
                        act.wait_ge(sem(kind + "_split"), was(kind + "_split") + i - 1)
                    elif kind == "q":
                        act.wait_ge(sem("k_split"), was("k_split") + 2 * QC)
                    nc.scalar.activation(stg[i % 2][:, 0:cn], ps[:, bank, 0:cn], ACT.Identity,
                                         bias=bqk[:, 1 if kind == "k" else 0, m:m + 1],
                                         scale=1.0 if kind == "k" else HD ** -0.5).then_inc(sem(kind + "_done"), 1)
                    if kind == "q" or L == 1:
                        if i >= 2:
                            act.wait_ge(sem(f"{kind}_out{i % 2}"), was(f"{kind}_out{i % 2}") + 16 * (i // 2))
                        elif kind == "q":
                            act.wait_ge(sem(f"k_out{i % 2}"), was(f"k_out{i % 2}") + 16 * QC)
                        nc.scalar.activation(stg_p[i % 2][:, 0, 0:cn], ps[:, bank, 0:cn], ACT.Identity,
                                             bias=bqk[:, 1 if kind == "k" else 0, m:m + 1],
                                             scale=1.0 if kind == "k" else HD ** -0.5).then_inc(sem(kind + "_first"), 1)
                act.wait_ge(sem("q_split"), was("q_split") + 2 * QC)
                act.wait_ge(sem("q_out0"), was("q_out0") + 16 * QC)
                act.wait_ge(sem("q_out1"), was("q_out1") + 16 * QC)

                def evac(n):
                    act.wait_ge(sem("pv_done"), was("pv_done") + n * KT + KT)
                    nc.scalar.activation(OT[:, bass.ds(n, 1), :].rearrange("p a c -> p (a c)"), ps[:, 7, :], ACT.Copy).then_inc(sem("ot_set"), 1)

                def sums(n):
                    act.wait_ge(sem("sum_full"), was("sum_full") + n + 1)
                    wait(act, sem("on_set"), was("on_set") + n)
                    nc.scalar.activation(rsum, ps[:, 4, :], ACT.Identity, bias=tiny[:, :]).then_inc(sem("sum_out"), 1)

                def exps(n, b):
                    for kt in range(KT):
                        kn = P if kt < KT - 1 else KLAST
                        for half in range(2):
                            v = 2 * kt + half
                            buf = (2 * KT * b + v) % 4
                            act.wait_ge(sem("sc_full"), was("sc_full") + n * 2 * KT + v + 1)
                            wait(act, sem("pv_done"), was("pv_done") + n * KT + kt - 1)
                            nc.scalar.activation(Pt[buf][0:kn, :], ps[0:kn, 2 * (v % 2):2 * (v % 2) + 2, :].rearrange("p b c -> p (b c)"),
                                                 ACT.Exp).then_inc(sem("p_set"), 1)
                            if not (isinstance(n, int) and n == 0):
                                if v == 1:
                                    evac(n - 1)
                                if v == 2 * M_AT + 1:
                                    sums(n - 1)

                exps(0, 0)
                exps(1, 1)
                with act.Fori(1, NIT // 2) as pair:
                    for b in range(2):
                        exps(2 * pair + b, b)
                evac(NIT - 1)
                sums(NIT - 1)
                if L == 0:
                    moe_act(act)
            final_act(act)

        def ln_stats(dve, link, src, var_sem, rstd_sem, out_sem, rstd_count=1):
            for t in range(TT):
                ins = nc.vector.bn_stats(bst[:, t, :], src[:, t, :])
            link(ins)
            link(nc.vector.tensor_tensor(lnt[0], bst[:, :, 1], bst[:, :, 4], ALU.add))
            nc.vector.tensor_tensor(lnt[2], bst[:, :, 1], bst[:, :, 4], ALU.subtract)
            link(nc.vector.tensor_tensor(lnt[3], bst[:, :, 2], bst[:, :, 5], ALU.add))
            link(nc.vector.tensor_tensor(lnt[4], lnt[2], lnt[2], ALU.mult))
            link(nc.vector.scalar_tensor_tensor(lnt[4], lnt[4], 64.0, lnt[3], ALU.mult, ALU.add))
            nc.vector.tensor_scalar(lnt[1], lnt[0], 0.5, None, ALU.mult)
            nc.vector.tensor_scalar(lnt[5], lnt[4], 1.0 / D, EPS, ALU.mult, ALU.add).then_inc(var_sem, 1)
            dve.wait_ge(rstd_sem, rstd_count)
            for t in range(TT):
                nc.vector.tensor_scalar(xn[:, t, :], src[:, t, :], lnt[1][:, t:t + 1], lnt[6][:, t:t + 1],
                                        ALU.subtract, ALU.mult).then_inc(out_sem, 1)

        def split(dve, link, was, kind, i, L):
            s = i % 2
            m, c = i // QC, i % QC
            cn = chunk(c)[1] if kind == "k" else CH
            dve.wait_ge(sem(kind + "_done"), was(kind + "_done") + i + 1)
            if kind == "k" and L == 0:
                link(nc.vector.tensor_tensor(stg[s][:, 0:cn], stg[s][:, 0:cn], keepB[:, chunk(c)[0]:chunk(c)[0] + cn], ALU.mult))
            if i >= 2:
                dve.wait_ge(sem(f"{kind}_out{s}"), was(f"{kind}_out{s}") + 16 * (i // 2))
            elif kind == "q":
                dve.wait_ge(sem(f"k_out{s}"), was(f"k_out{s}") + 16 * QC)
            if kind == "k" and L == 0:
                link(nc.vector.tensor_copy(stg_p[s][:, 0, 0:cn], stg[s][:, 0:cn]))
            elif kind == "k":
                dve.wait_ge(sem("k_first"), i + 1)
            else:
                dve.wait_ge(sem("q_first"), was("q_first") + i + 1)
            link(nc.vector.tensor_tensor(stg_r[s][:, 0:cn], stg[s][:, 0:cn], stg_p[s][:, 0, 0:cn], ALU.subtract))
            link(nc.vector.tensor_copy(stg_p[s][:, 1, 0:cn], stg_r[s][:, 0:cn]))
            nc.vector.tensor_tensor(stg_p[s][:, 2, 0:cn], stg_r[s][:, 0:cn], stg_p[s][:, 1, 0:cn], ALU.subtract)\
                .then_inc(sem(kind + "_split"), 1)

        def moe_dve(dve, link):
            dve.wait_ge(sem("x_add"), TT)
            ln_stats(dve, link, x_sb, sem("var_set_m"), sem("rstd_set_m"), sem("xn_set_m"))
            dve.wait_ge(sem("xn_set_m"), TT)
            for t in range(TT):
                ins = nc.vector.bn_stats(bst[:, t, :], xn[:, t, :])
            link(ins)
            nc.vector.tensor_tensor(lnt[2], bst[:, :, 1], bst[:, :, 4], ALU.subtract)
            nc.vector.tensor_tensor(lnt[3], bst[:, :, 2], bst[:, :, 5], ALU.add)
            link(nc.vector.tensor_tensor(lnt[0], bst[:, :, 1], bst[:, :, 4], ALU.add))
            link(nc.vector.tensor_tensor(lnt[4], lnt[2], lnt[2], ALU.mult))
            link(nc.vector.scalar_tensor_tensor(lnt[4], lnt[4], 64.0, lnt[3], ALU.mult, ALU.add))
            link(nc.vector.tensor_scalar(st[:, :, 0], lnt[0], 0.5, None, ALU.mult))
            link(nc.vector.tensor_tensor(lnt[9], st[:, :, 0], st[:, :, 0], ALU.mult))
            nc.vector.scalar_tensor_tensor(lnt[8], lnt[9], float(D), lnt[4], ALU.mult, ALU.add).then_inc(sem("var2_set"), 1)
            nc.vector.tensor_scalar(lnt[7], lnt[4], 1.0 / (D - 1), None, ALU.mult).then_inc(sem("var2_set"), 1)
            nc.vector.tensor_reduce(st[:, :, 2], xn, AX.X, ALU.min).then_inc(sem("st_set"), 1)
            nc.vector.tensor_reduce(st[:, :, 3], xn, AX.X, ALU.max).then_inc(sem("st_set"), 1)
            for t0, t1 in ((0, 14), (14, TT)):
                near = PB[:, 0:(t1 - t0) * D]
                link(nc.vector.tensor_scalar(near, R2[:, t0 * D:t1 * D], -1e-6, None, ALU.is_gt))
                link(nc.vector.scalar_tensor_tensor(near, R2[:, t0 * D:t1 * D], 1e-6, near, ALU.is_lt, ALU.mult))
                link(nc.vector.tensor_reduce(lnt[9][:, t0:t1], near.rearrange("p (t d) -> p t d", d=D), AX.X, ALU.add))
            nc.vector.tensor_scalar(st[:, :, 5], lnt[9], 1.0 / D, None, ALU.mult).then_inc(sem("st_set"), 1)
            for c in range(QC):
                dve.wait_ge(sem("stt_full"), c + 1)
                nc.vector.tensor_copy(stT[:, c * CH:(c + 1) * CH], ps[0:6, c, :]).then_inc(sem("stt_done"), 1)
            dve.wait_ge(sem("lg_full"), 1)
            lgp = ps[:, 0, :].rearrange("p (t e) -> p t e", e=E)
            bc = lambda v: v.rearrange("p (t o) -> p t o", o=1).to_broadcast([P, TT, E])
            link(nc.vector.tensor_reduce(lnt[0], lgp, AX.X, ALU.max))
            nc.vector.tensor_tensor(lg, lgp, bc(lnt[0]), ALU.subtract).then_inc(sem("lg_sub"), 1)
            dve.wait_ge(sem("lg_exp"), 1)
            link(nc.vector.tensor_reduce(lnt[1], lg, AX.X, ALU.add))
            link(nc.vector.reciprocal(lnt[2], lnt[1]))
            link(nc.vector.tensor_tensor(prb, lg, bc(lnt[2]), ALU.mult))
            for t in range(TT):
                ins = nc.vector.max(top8[:, t, :], prb[:, t, :])
            link(ins)
            for t in range(TT):
                ins = nc.vector.max_index(topi[:, t, :], top8[:, t, :], prb[:, t, :])
            link(ins)
            link(nc.vector.tensor_tensor(den, top8[:, :, 0], top8[:, :, 1], ALU.add))
            nc.vector.reciprocal(den, den).then_inc(sem("den_set"), 1)
            link(nc.vector.tensor_copy(topf, topi[:, :, 0:2]))
            dve.wait_ge(sem("iota_set"), 1)
            nc.vector.tensor_tensor(hit1, iot, topf[:, :, 0:1].to_broadcast([P, TT, E]), ALU.is_equal)
            link(nc.vector.tensor_tensor(hit2, iot, topf[:, :, 1:2].to_broadcast([P, TT, E]), ALU.is_equal))
            link(nc.vector.tensor_tensor(hit1, hit1, hit2, ALU.add))
            link(nc.vector.tensor_tensor(prb, prb, hit1, ALU.mult))
            nc.vector.scalar_tensor_tensor(prb, hit1, -1.0, prb, ALU.add, ALU.add).then_inc(sem("score_set"), 1)
            dve.wait_ge(sem("sct_full"), 1)
            link(nc.vector.tensor_copy(scT, ps[0:E, 1:5, :].rearrange("p b c -> p (b c)")))
            src, dst = scT, scT2
            for r in range(ROUNDS):
                link(nc.vector.max(vals[:, 8 * r:8 * r + 8], src))
                ins = nc.vector.max_index(idx8[:, 8 * r:8 * r + 8], vals[:, 8 * r:8 * r + 8], src)
                if r < ROUNDS - 1:
                    ins = nc.vector.match_replace(dst, vals[:, 8 * r:8 * r + 8], src, -2.0)
                link(ins)
                src, dst = dst, src
            nc.vector.tensor_copy(idxf, idx8).then_inc(sem("top_set"), 1)
            dve.wait_ge(sem("topT_full"), 1)
            nc.vector.tensor_scalar(valT, ps[0:CAP, 5, 0:E], 0.0, None, ALU.max).then_inc(sem("idx_set"), 1)
            nc.vector.tensor_copy(idxT, ps[0:CAP, 5, E:2 * E]).then_inc(sem("idx_set"), 1)
            dve.wait_ge(sem("idx_set"), 2)

            def rows(r, s):
                e = r * SLOTS + s
                dve.wait_ge(sem(f"xe_in{s}"), 16 * r + 16)
                nc.vector.tensor_tensor(wcol[:, s:s + 1], valT[:, bass.ds(e, 1)], xe[s][:, D:D + 1], ALU.mult).then_inc(sem("w_set"), 1)
                dve.wait_ge(sem("xe_t"), e + 1)
                nc.vector.tensor_copy(xeT[s % 2], ps[:, 5, 0:2 * CAP].rearrange("p (k c) -> p k c", k=2)).then_inc(sem("xeT_set"), 1)

            def hidden(r, s):
                b = s % 2
                e = r * SLOTS + s
                dve.wait_ge(sem("silu_set"), e + 1)
                nc.vector.tensor_tensor(hh[b][:, 0:INTER], sg[b][:, 0:INTER], ps[0:CAP, 2 + b, :], ALU.mult)
                nc.vector.scalar_tensor_tensor(hh[b][:, INTER:HALL], ps[0:CAP, 4, A_INTER:2 * A_INTER], ADAPTER_SCALE,
                                               sg[b][:, INTER:HALL], ALU.mult, ALU.mult).then_inc(sem(f"hh_set{b}"), 1)
                dve.wait_ge(sem("hhT_full"), e + 1)
                nc.vector.tensor_copy(hhT[b], ps[:, 6, 0:5 * CAP].rearrange("p (k c) -> p k c", k=5)).then_inc(sem("hhT_set"), 1)

            def output(r, s):
                b = s % 2
                e = r * SLOTS + s
                dve.wait_ge(sem("dn_done"), e + 1)
                dve.wait_ge(sem("w_set"), e + 1)
                wait(dve, sem(f"sc_done{b}"), 16 * (r * 2 + s // 2))
                nc.vector.tensor_scalar(ye[b], ps[0:CAP, 7, 0:D], wcol[:, s:s + 1], None, ALU.mult).then_inc(sem("ye_set"), 1)

            def round_(r, last):
                for s in range(SLOTS):
                    hidden(r, s)
                    if not (last and s + 2 >= SLOTS):
                        rows(r + (s + 2) // SLOTS, (s + 2) % SLOTS)
                    output(r, s)

            rows(0, 0)
            rows(0, 1)
            round_(0, False)
            with dve.Fori(1, E // SLOTS - 1) as r:
                round_(r, False)
            round_(E // SLOTS - 1, True)

        def final_dve(dve, link):
            def round_fp8(v, t1, out):
                link(nc.vector.tensor_scalar(t1.bitcast(I32), v.bitcast(I32), 0x7F800000, None, ALU.bitwise_and))
                link(nc.vector.tensor_scalar(t1, t1, 2.0 ** -6, 1.5 * 2.0 ** 20, ALU.max, ALU.mult))
                link(nc.vector.tensor_tensor(v, v, t1, ALU.add))
                link(nc.vector.tensor_tensor(v, v, t1, ALU.subtract))
                link(nc.vector.tensor_scalar(t1.bitcast(I32), v.bitcast(I32), 0x7FFFFFFF, None, ALU.bitwise_and))
                link(nc.vector.tensor_scalar(t1, t1, 2.0 ** 119, 0.2 * 2.0 ** 127, ALU.mult, ALU.add))
                return nc.vector.scalar_tensor_tensor(out, t1, 0.0, v, ALU.mult, ALU.add)

            dve.wait_ge(sem("x_add"), 2 * TT)
            ln_stats(dve, link, x_sb, sem("var_setf"), sem("rstd_setf"), sem("xn_setf"))
            dve.wait_ge(sem("f_in"), 16 * 4)
            link(nc.vector.tensor_tensor(fsc[:, 2:3], fsc[:, 0:1], fsc[:, 1:2], ALU.mult))
            link(nc.vector.reciprocal(fsc[:, 0:2], fsc[:, 0:2]))
            link(nc.vector.tensor_tensor(fk.rearrange("p k o -> p (k o)"), fkb.rearrange("p k o -> p (k o)"), fsc[:, 1:2].to_broadcast([P, 2 * D]), ALU.mult))
            round_fp8(fk.rearrange("p k o -> p (k o)"), fa[:, 0:512], fkq.rearrange("p k o -> p (k o)")).then_inc(sem("fk_set"), 1)
            dve.wait_ge(sem("fk_set"), 1)
            dve.wait_ge(sem("xn_setf"), TT)
            NPC = 4
            w4 = TT * D // NPC
            for c in range(NPC):
                part = slice(c * w4, (c + 1) * w4)
                link(nc.vector.tensor_copy(fxb[:, part], R2[:, part]))
                link(nc.vector.tensor_tensor(fx[:, part], fxb[:, part], fsc[:, 0:1].to_broadcast([P, w4]), ALU.mult))
                round_fp8(fx[:, part], fa[:, part], fxb[:, part]).then_inc(sem("fx_set"), 1)
            for t in range(TT):
                yb = fyb[t % 2]
                dve.wait_ge(sem("y_full"), t + 1)
                link(nc.vector.tensor_scalar(yb, ps[:, 4 + t % 4, 0:D], fsc[:, 2:3], None, ALU.mult))
                link(nc.vector.tensor_tensor(yb, yb, fbb, ALU.add))
                nc.vector.tensor_tensor(x_sb[:, t, :], x_sb[:, t, :], yb, ALU.add).then_inc(sem("x_out"), 1)

        @block.vector
        def _(dve):
            cnt = [0]

            def link(ins):
                cnt[0] += 1
                ins.then_inc(sem("dve_chain"), 1)
                dve.wait_ge(sem("dve_chain"), cnt[0])

            for L in range(2):
                was = lambda n, L=L: L * PER_LAYER[n]
                if L == 0:
                    dve.wait_ge(sem("keep_in"), 16)
                    dve.wait_ge(sem("fillc"), 4)
                    link(nc.vector.tensor_copy(keepB, keepU))
                    link(nc.vector.tensor_scalar(fillr[96:P, :], keepB[96:P, :], -1.0, 1.0, ALU.mult, ALU.add))
                    nc.vector.tensor_scalar(fillr[96:P, :], fillr[96:P, :], fillc[96:P, L:L + 1], None, ALU.mult).then_inc(sem("fill_set"), 1)
                    dve.wait_ge(sem("x_in"), 64)
                else:
                    dve.wait_ge(sem("left_out_in"), 16)
                    nc.vector.tensor_scalar(fillr[96:P, :], keepB[96:P, :], fillc[96:P, L:L + 1], None, ALU.mult).then_inc(sem("fill_set"), 1)
                    dve.wait_ge(sem("x_back"), 16)
                ln_stats(dve, link, x_sb, sem("var_set"), sem("rstd_set"), sem("xn_set"), L + 1)
                for i in range(2 * QC):
                    split(dve, link, was, "k", i, L)
                for i in range(2 * QC):
                    split(dve, link, was, "q", i, L)
                dve.wait_ge(sem("b_in"), was("b_in") + 64)
                dve.wait_ge(sem("v_ones"), was("v_ones") + 1)
                for i in range(KT):
                    kn = P if i < KT - 1 else KLAST
                    pos = prep_units().index(("v", i))
                    dve.wait_ge(sem("v_full"), was("v_full") + i + 1)
                    for g in range(HG):
                        ins = nc.vector.tensor_tensor(
                            Vp[0:kn, g, i * HPG:(i + 1) * HPG, 0:HD],
                            ps[0:kn, pos % 8, g * 64:(g + 1) * 64].rearrange("p (u c) -> p u c", c=HD),
                            bvB[0:kn, g * 64:(g + 1) * 64].rearrange("p (u c) -> p u c", c=HD), ALU.add)
                    ins.then_inc(sem("v_done"), 1)

                def mx_red(n, u):
                    what, i, q = MX[u]
                    dve.wait_ge(sem("mx_full"), was("mx_full") + n * NMX + u + 1)
                    if what == "A":
                        ins = nc.vector.tensor_reduce(mxs[:, i * 4 + q:i * 4 + q + 1], ps[:, 4:6, :].rearrange("p b c -> p (b c)"), AX.X, ALU.max)
                    elif what == "B":
                        ins = nc.vector.tensor_reduce(mxs[:, 16 + i * 4 + q:16 + i * 4 + q + 1], ps[:, 6, :], AX.X, ALU.max)
                    else:
                        ins = nc.vector.tensor_reduce(mxs[:, 32 + i * 4:32 + i * 4 + 4],
                                                      ps[:, 6, 0:4 * KLAST].rearrange("p (q c) -> p q c", c=KLAST), AX.X, ALU.max)
                    ins.then_inc(sem("mx_done"), 1)

                def m_split(n):
                    dve.wait_ge(sem("mx_done"), was("mx_done") + n * NMX + NMX)
                    nc.vector.tensor_reduce(negm[:, :], mxs[:, :].rearrange("p (w u) -> p u w", w=3), AX.X, ALU.max,
                                            negate=True).then_inc(sem("negm_set"), 1)
                    dve.wait_ge(sem("m_full"), was("m_full") + n + 1)
                    wait(dve, sem("m_out"), was("m_out") + 16 * n)
                    c4 = n * 4
                    nc.vector.tensor_scalar(mrest[:, :], ps[0:16, 6, 0:P], HUGE_CUT, None, ALU.min).then_inc(sem("mc"), 1)
                    dve.wait_ge(sem("mc"), was("mc") + c4 + 1)
                    nc.vector.tensor_copy(mparts[:, 0, :], mrest[:, :]).then_inc(sem("mc"), 1)
                    dve.wait_ge(sem("mc"), was("mc") + c4 + 2)
                    nc.vector.tensor_tensor(mrest[:, :], mrest[:, :], mparts[:, 0, :], ALU.subtract).then_inc(sem("mc"), 1)
                    dve.wait_ge(sem("mc"), was("mc") + c4 + 3)
                    nc.vector.tensor_copy(mparts[:, 1, :], mrest[:, :]).then_inc(sem("mc"), 1)
                    dve.wait_ge(sem("mc"), was("mc") + c4 + 4)
                    nc.vector.tensor_tensor(mparts[:, 2, :], mrest[:, :], mparts[:, 1, :], ALU.subtract).then_inc(sem("m_split"), 1)

                for u in range(NMX):
                    mx_red(0, u)
                m_split(0)
                for u in range(AHEAD2):
                    mx_red(1, u)

                def invert(n, piece):
                    cols = slice(piece * CH // PIECES, (piece + 1) * CH // PIECES)
                    if piece == 0:
                        dve.wait_ge(sem("sum_out"), was("sum_out") + n + 1)
                    ins = nc.vector.reciprocal(rsum[:, cols], rsum[:, cols])
                    if piece == PIECES - 1:
                        ins.then_inc(sem("inv_set"), 1)

                def iteration(n, nxt, nxt2):
                    some = not (isinstance(n, int) and n == 0)
                    more = not (isinstance(n, int) and n <= 1)
                    piece = AHEAD2 // PER_TILE
                    for u in range(AHEAD2, NMX):
                        if nxt:
                            mx_red(n + 1, u)
                        if u % PER_TILE == PER_TILE - 1 and piece < PIECES:
                            if more:
                                invert(n - 2, piece)
                            piece += 1
                    if nxt:
                        m_split(n + 1)
                    for u in range(AHEAD2):
                        if nxt2:
                            mx_red(n + 2, u)
                        if u % PER_TILE == PER_TILE - 1 and some:
                            invert(n - 1, u // PER_TILE)

                iteration(0, True, True)
                iteration(1, True, True)
                with dve.Fori(2, NIT - 2) as n:
                    iteration(n, True, True)
                iteration(NIT - 2, True, False)
                iteration(NIT - 1, False, False)
                for piece in range(AHEAD2 // PER_TILE, PIECES):
                    invert(NIT - 2, piece)
                for piece in range(PIECES):
                    invert(NIT - 1, piece)
                dve.wait_ge(sem("bo_add"), was("bo_add") + 1)
                for t in range(TT):
                    dve.wait_ge(sem("o_full"), was("o_full") + t + 1)
                    nc.vector.tensor_tensor(x_sb[:, t, :], x_sb[:, t, :], ps[:, O_BANKS[t % len(O_BANKS)], 0:D], ALU.add).then_inc(sem("x_add"), 1)
                if L == 0:
                    moe_dve(dve, link)
            final_dve(dve, link)

_T = {"L0_ffn_w_up": "upT", "L0_ffn_w_down": "dnT", "L0_ffn_a_up": "aupT", "L0_ffn_a_down": "adnT"}


def laid_out(inputs):
    import numpy as np
    got = {"x": inputs["x"], "ctxT": inputs["ctx_1024"][0].T, "mask0": inputs["mask_BxS2_bf1"],
           "mask1": inputs["mask_1x1xSxS2_bk1"], "mask1T": inputs["mask_1x1xSxS2_bk1"][0, 0].T}
    for L in range(2):
        for n in "qkvo":
            got[f"L{L}_xattn_W{n}"] = inputs[f"L{L}_xattn_W{n}"].T
            got[f"L{L}_xattn_b{n}"] = inputs[f"L{L}_xattn_b{n}"]
    got["r1T"] = inputs["L0_ffn_r1_w"][:, :D].T
    got["r1sT"] = inputs["L0_ffn_r1_w"][:, D:].T
    got["r2T"] = inputs["L0_ffn_r2_w"].T
    got["L0_ffn_r1_b"] = inputs["L0_ffn_r1_b"]
    for n, t in _T.items():
        got[t] = inputs[n].transpose(0, 2, 1)
    got["fk"] = inputs["L1_ffn_kernel"]
    got["s_in"] = inputs["L1_ffn_input_scale"]
    got["s_k"] = inputs["L1_ffn_kernel_scale"]
    got["fbias"] = inputs["L1_ffn_bias"]
    return {n: np.ascontiguousarray(v) for n, v in got.items()}


def kernel(**inputs):
    import concourse.bacc as _bacc
    from concourse import mybir as _mybir
    from concourse.bass_utils import run_bass_kernel_spmd as _run

    nc = _bacc.Bacc("TRN2", target_bir_lowering=False, num_devices=1)
    arrays, args = {}, {}
    for name, v in laid_out(inputs).items():
        arrays[f"in_{name}_dram"] = v
        args[name] = nc.dram_tensor(f"in_{name}_dram", v.shape, _mybir.dt.from_np(v.dtype), kind="ExternalInput").ap()
    args["out"] = nc.dram_tensor("out_0_dram", (1, T, D), F32, kind="ExternalOutput").ap()
    build(nc, args)
    r = _run(nc, [arrays], core_ids=[0])
    return r.results[0]["out_0_dram"]
```
